# Optimizing a Trainium2 kernel written in Bass

```python
import numpy as np
import jax
import jax.numpy as jnp

def _softmax(x, axis=-1):
    return jax.nn.softmax(x, axis=axis)
def _gelu(x):
    return jax.nn.gelu(x, approximate=True)
def _silu(x):
    return jax.nn.silu(x)
def _sigmoid(x):
    return jax.nn.sigmoid(x)
def _layernorm(x, axis=-1, eps=1e-5):
    m = jnp.mean(x, axis=axis, keepdims=True)
    v = jnp.var(x, axis=axis, keepdims=True)
    return (x - m) / jnp.sqrt(v + eps)
def _scatter_add(tgt, idx, src, axis=0):
    return tgt.at[idx].add(src)
def _segment_sum(src, seg, n):
    return jax.ops.segment_sum(src, seg, n)

kernel_name = 'mk_conv_preact_d2_conv_nchw128_9fb589'

def setup_inputs(seed: int = 0):
    np.random.seed(seed)
    _w = jnp.asarray
    def _rec_inputs():
        import jax
        import jax.numpy as jnp
        _gk = jax.random.key(seed)
        x = -0.0001732 + 1 * jax.random.normal(jax.random.fold_in(_gk, 1), (16, 128, 48, 48), jnp.float32)
        return x
    x = _rec_inputs()
    def _L0_conv_setup():
        import jax, jax.numpy as jnp
        import numpy as np
        from jax import lax
        C, H, W, N = (128, 48, 48, 16)
        SHIFT_W = 1
        SHIFT_C = 1

        def _forward(x, p5_w, w6, w8, w10):
            n, c, h, w = x.shape
            hw = h * w
            inv_sqrt_c = np.float32(1.0 / np.sqrt(c))
            inv_sqrt_hw = np.float32(1.0 / np.sqrt(hw))
            t1 = x.max(axis=1)
            t2 = -x
            t4 = jnp.maximum(t2, jnp.roll(t2, SHIFT_W, axis=3))
            t5 = p5_w * t4
            t6 = jnp.einsum('oc,nchw->nohw', w6, t5)
            t7 = jnp.einsum('ncp,ncq->npq', t6.reshape(n, c, hw), x.reshape(n, c, hw)) * inv_sqrt_c
            t8 = lax.conv_general_dilated(t1[:, None, :, :], w8, window_strides=(1, 1), padding=((0, 0), (6, 6)), rhs_dilation=(1, 3), dimension_numbers=('NCHW', 'OIHW', 'NCHW'))
            pad = jnp.pad(t8, ((0, 0), (0, 0), (2, 2), (0, 0)))
            t9 = jnp.stack([pad[:, :, 2 * k:2 * k + h, :] for k in range(3)], axis=2)
            t10 = jnp.einsum('oc,nchw->nohw', w10, t9.reshape(n, 3 * c // 2, h, w))
            t11 = jnp.roll(t10, SHIFT_C, axis=1)
            t12 = jnp.maximum(x, t11)
            t13 = jnp.einsum('npq,ncp->nqc', t7, t12.reshape(n, c, hw)) * inv_sqrt_hw
            return t13.reshape(n, h, w, c).transpose(0, 3, 1, 2)
        key = jax.random.key(seed)
        k1, k2, k3, k4, k5 = jax.random.split(key, 5)
        x = jax.random.normal(k1, (N, C, H, W), dtype=jnp.float32)
        p5_w = 0.02 * jax.random.truncated_normal(k2, -2.0, 2.0, (1, C, H, W), dtype=jnp.float32)
        w6 = jax.random.normal(k3, (C, C), dtype=jnp.float32) / np.float32(np.sqrt(C))
        w8 = jax.random.normal(k4, (C // 2, 1, 1, 5), dtype=jnp.float32) / np.float32(np.sqrt(5))
        w10 = jax.random.normal(k5, (C, 3 * C // 2), dtype=jnp.float32) / np.float32(np.sqrt(3 * C // 2))
        return {'x': x, 'p5_w': p5_w, 'w6': w6, 'w8': w8, 'w10': w10}
    _L0_conv_all = _L0_conv_setup()
    _L0_conv_in = {k: v for k, v in _L0_conv_all.items() if k in ('p5_w', 'w6', 'w8', 'w10', )}
    del _L0_conv_all

    def _L1_conv_setup():
        import jax, jax.numpy as jnp
        import numpy as np
        C = 128
        HID = 4 * C
        K = 7
        PAD = K // 2
        B, T, F = (4, 512, 128)
        LN_EPS = 1e-05
        LS_INIT = 0.01
        key = jax.random.key(seed)
        ks = jax.random.split(key, 4)
        x = jax.random.normal(ks[0], (B, C, T, F), dtype=jnp.float32)
        dw_w = jax.random.normal(ks[1], (C, 1, K, K), dtype=jnp.float32) * (1.0 / K)
        dw_b = jnp.zeros((C,), dtype=jnp.float32)
        ln_g = jnp.ones((C,), dtype=jnp.float32)
        ln_b = jnp.zeros((C,), dtype=jnp.float32)
        w1 = jax.random.normal(ks[2], (HID, C), dtype=jnp.float32) * (1.0 / np.sqrt(C))
        b1 = jnp.zeros((HID,), dtype=jnp.float32)
        w2 = jax.random.normal(ks[3], (C, HID), dtype=jnp.float32) * (1.0 / np.sqrt(HID))
        b2 = jnp.zeros((C,), dtype=jnp.float32)
        ls = jnp.full((C,), LS_INIT, dtype=jnp.float32)
        return {'x': x, 'dw_w': dw_w, 'dw_b': dw_b, 'ln_g': ln_g, 'ln_b': ln_b, 'w1': w1, 'b1': b1, 'w2': w2, 'b2': b2, 'ls': ls}
    _L1_conv_all = _L1_conv_setup()
    _L1_conv_in = {k: v for k, v in _L1_conv_all.items() if k in ('dw_w', 'dw_b', 'ln_g', 'ln_b', 'w1', 'b1', 'w2', 'b2', 'ls', )}
    del _L1_conv_all

    return {
        "x": x,
        "L0_conv_p5_w": _L0_conv_in["p5_w"],
        "L0_conv_w6": _L0_conv_in["w6"],
        "L0_conv_w8": _L0_conv_in["w8"],
        "L0_conv_w10": _L0_conv_in["w10"],
        "L1_conv_dw_w": _L1_conv_in["dw_w"],
        "L1_conv_dw_b": _L1_conv_in["dw_b"],
        "L1_conv_ln_g": _L1_conv_in["ln_g"],
        "L1_conv_ln_b": _L1_conv_in["ln_b"],
        "L1_conv_w1": _L1_conv_in["w1"],
        "L1_conv_b1": _L1_conv_in["b1"],
        "L1_conv_w2": _L1_conv_in["w2"],
        "L1_conv_b2": _L1_conv_in["b2"],
        "L1_conv_ls": _L1_conv_in["ls"],
    }

def reference(x, L0_conv_p5_w, L0_conv_w6, L0_conv_w8, L0_conv_w10, L1_conv_dw_w, L1_conv_dw_b, L1_conv_ln_g, L1_conv_ln_b, L1_conv_w1, L1_conv_b1, L1_conv_w2, L1_conv_b2, L1_conv_ls):
    import jax
    import jax.numpy as jnp
    def _L0_conv_ref(x, p5_w, w6, w8, w10):
        import jax, jax.numpy as jnp
        import numpy as np
        from jax import lax
        C, H, W, N = (128, 48, 48, 16)
        SHIFT_W = 1
        SHIFT_C = 1

        def _forward(x, p5_w, w6, w8, w10):
            n, c, h, w = x.shape
            hw = h * w
            inv_sqrt_c = np.float32(1.0 / np.sqrt(c))
            inv_sqrt_hw = np.float32(1.0 / np.sqrt(hw))
            t1 = x.max(axis=1)
            t2 = -x
            t4 = jnp.maximum(t2, jnp.roll(t2, SHIFT_W, axis=3))
            t5 = p5_w * t4
            t6 = jnp.einsum('oc,nchw->nohw', w6, t5)
            t7 = jnp.einsum('ncp,ncq->npq', t6.reshape(n, c, hw), x.reshape(n, c, hw)) * inv_sqrt_c
            t8 = lax.conv_general_dilated(t1[:, None, :, :], w8, window_strides=(1, 1), padding=((0, 0), (6, 6)), rhs_dilation=(1, 3), dimension_numbers=('NCHW', 'OIHW', 'NCHW'))
            pad = jnp.pad(t8, ((0, 0), (0, 0), (2, 2), (0, 0)))
            t9 = jnp.stack([pad[:, :, 2 * k:2 * k + h, :] for k in range(3)], axis=2)
            t10 = jnp.einsum('oc,nchw->nohw', w10, t9.reshape(n, 3 * c // 2, h, w))
            t11 = jnp.roll(t10, SHIFT_C, axis=1)
            t12 = jnp.maximum(x, t11)
            t13 = jnp.einsum('npq,ncp->nqc', t7, t12.reshape(n, c, hw)) * inv_sqrt_hw
            return t13.reshape(n, h, w, c).transpose(0, 3, 1, 2)
        return _forward(x, p5_w, w6, w8, w10)

    def _L1_conv_ref(x, dw_w, dw_b, ln_g, ln_b, w1, b1, w2, b2, ls):
        import jax, jax.numpy as jnp
        import numpy as np
        C = 128
        HID = 4 * C
        K = 7
        PAD = K // 2
        B, T, F = (4, 512, 128)
        LN_EPS = 1e-05
        LS_INIT = 0.01
        y = jax.lax.conv_general_dilated(x, dw_w, window_strides=(1, 1), padding=[(PAD, PAD), (PAD, PAD)], feature_group_count=x.shape[1], dimension_numbers=('NCHW', 'OIHW', 'NCHW'))
        y = y + dw_b[None, :, None, None]
        y = jnp.transpose(y, (0, 2, 3, 1))
        mu = jnp.mean(y, axis=-1, keepdims=True)
        var = jnp.mean(jnp.square(y - mu), axis=-1, keepdims=True)
        y = (y - mu) * jax.lax.rsqrt(var + LN_EPS) * ln_g + ln_b
        h = jax.nn.gelu(jnp.einsum('btfc,hc->btfh', y, w1) + b1)
        y = jnp.einsum('btfh,ch->btfc', h, w2) + b2
        y = y * ls
        return jnp.transpose(y, (0, 3, 1, 2))

    def _gn(v, G=32, eps=1e-5):
        B_, C_, H_, W_ = v.shape
        g = v.reshape(B_, G, C_ // G, H_, W_)
        m = jnp.mean(g, axis=(2, 3, 4), keepdims=True)
        s = jnp.var(g, axis=(2, 3, 4), keepdims=True)
        return ((g - m) / jnp.sqrt(s + eps)).reshape(v.shape)

    def _ln_c(v, eps=1e-6):
        m = jnp.mean(v, axis=1, keepdims=True)
        s = jnp.var(v, axis=1, keepdims=True)
        return (v - m) / jnp.sqrt(s + eps)

    def _ln_t(v, eps=1e-5):
        m = jnp.mean(v, axis=-1, keepdims=True)
        s = jnp.var(v, axis=-1, keepdims=True)
        return (v - m) / jnp.sqrt(s + eps)

    def _to_tokens(v):
        B_, C_, H_, W_ = v.shape
        return v.reshape(B_, C_, H_ * W_).transpose(0, 2, 1)
    def _from_tokens(t, like):
        B_, C_, H_, W_ = like.shape
        return t.transpose(0, 2, 1).reshape(B_, C_, H_, W_)

    x = x + _L0_conv_ref(_gn(x), L0_conv_p5_w, L0_conv_w6, L0_conv_w8, L0_conv_w10)
    x = x + _L1_conv_ref(_gn(x), L1_conv_dw_w, L1_conv_dw_b, L1_conv_ln_g, L1_conv_ln_b, L1_conv_w1, L1_conv_b1, L1_conv_w2, L1_conv_b2, L1_conv_ls)
    return x


_drawn_inputs = setup_inputs


def setup_inputs(seed=0):
    import zlib

    import numpy as np

    out = dict(_drawn_inputs(seed))
    spreads = {'L1_conv_dw_b': (0.0, 0.8),
     'L1_conv_ln_g': (1.0, 0.6),
     'L1_conv_ln_b': (0.0, 0.8),
     'L1_conv_b1': (0.0, 0.8),
     'L1_conv_b2': (0.0, 0.8),
     'L1_conv_ls': (0.009999999776482582, 0.6)}
    factors = {'L1_conv_dw_w': 8.0, 'L1_conv_w1': 8.0, 'L1_conv_w2': 8.0}
    for name, (base, spread) in spreads.items():
        noise = np.random.default_rng([zlib.crc32(name.encode()), seed]).standard_normal(out[name].shape)
        drawn = base * np.exp(spread * noise) if base else spread * noise
        out[name] = jnp.asarray(drawn.astype(out[name].dtype))
    for name, factor in factors.items():
        out[name] = (out[name] * factor).astype(out[name].dtype)
    return out
```

```python
from contextlib import ExitStack

import concourse.bass as bass
from concourse import mybir

F32 = mybir.dt.float32
ALU = mybir.AluOpType
ACT = mybir.ActivationFunctionType
AX_X = mybir.AxisListType.X


def build(nc, x, p5_w, w6t, w8, w10t, dw_rev, dw_b, ln_g, ln_b, w1t, b1, w2t, b2, ls, ident_in, gmat_in, out):
    N, C, HW = x.shape
    W = H = 48
    P = 128
    GI = 8
    NG = N // GI
    XS = 3
    CH = 384
    NCH = HW // CH
    NT = HW // P
    NB = NT // NCH
    CHR = CH // W
    PIECES = [(0, 0, 2, W), (0, 2 * W, 1, 32), (1, 0, 1, 16), (1, 16, 2, W), (1, 16 + 2 * W, 1, 16), (2, 0, 1, 32), (2, 32, 2, W)]
    HID = w1t.shape[1]
    NJ = HID // P
    HALF, HALO = W // 2, 3
    PW = HALF + 2 * HALO
    TR = 4
    TP = TR * PW
    TH = H // TR
    TI = 2 * TH
    TG = GI * TI
    K = 7
    KC = K // 2
    TAPS_H, TAPS_W = 3, 5
    NTAP = TAPS_H * TAPS_W
    T1W, T1H = W + 12, H + 4
    RL = 4 * TP
    TB = 3 * TP
    QC = 4
    UC = 2 * QC
    NK = 3
    SR = H // NK
    ST = SR // TR
    SP_ = SR * HALF
    GN_EPS, LN_EPS = 1e-5, 1e-5
    SCALE = -1.0 / (float(C) ** 0.5 * float(HW) ** 0.5)
    assert PW * KC + KC <= TP and SP_ == CH and 2 * SP_ * NK == HW

    t1pad = nc.dram_tensor("t1pad", (T1H, T1W), F32, kind="Internal")
    rvec = nc.dram_tensor("rvec", (C, RL), F32, kind="Internal")
    x1_dram = nc.dram_tensor("x1_dram", (N, C, HW), F32, kind="Internal").ap()

    with ExitStack() as ctx:
        def sb(name, shape):
            return ctx.enter_context(nc.sbuf_tensor(name, shape, F32))

        def sem(name):
            return ctx.enter_context(nc.semaphore(name))

        tiles = sb("tiles", [TP, C, TG])
        xin = sb("xin", [P, XS * HW])
        xn = sb("xn", [P, HW])
        t5 = sb("t5", [P, HW])
        p5 = sb("p5", [P, HW])
        xT = sb("xT", [P, HW])
        t5T = sb("t5T", [P, HW])
        xpad = sb("xpad", [P, 2, H, PW])
        shared = sb("shared", [P, UC * TB])
        ident = sb("ident", [P, P])
        gmat = sb("gmat", [P, P])
        w6s = sb("w6s", [P, P])
        wcT = sb("wcT", [NTAP, P])
        w1s = sb("w1s", [P, HID])
        w2s = sb("w2s", [P, NJ, P])
        dwb = sb("dwb", [TP, C])
        vecs = sb("vecs", [P, 12])
        m_sb = sb("m_sb", [P, P])
        g_sb = sb("g_sb", [P, P])
        gi_sb = sb("gi_sb", [P, P])
        t1 = sb("t1", [P, NT])
        t1row = sb("t1row", [NT, P])
        st1 = sb("st1", [P, NCH, 6])
        st2 = sb("st2", [P, NCH, 6])
        gn1 = sb("gn1", [P, 8])
        gn2 = sb("gn2", [P, 8])
        kept = sb("kept", [P, 2])
        cst = sb("cst", [P, 1])
        lnst = sb("lnst", [TP, 2 * ST, 6])
        lnmv = sb("lnmv", [TP, 2 * ST, 2])
        lnr = sb("lnr", [TP, 2, 2 * ST])
        minus_half = sb("minus_half", [P, 2 * ST])
        ps = ctx.enter_context(nc.psum_tensor("ps", [P, 8, 512], F32))

        taps = shared[0:NTAP, 0:HW]
        normed = shared[0:TP, 0:2 * ST * C].rearrange("p (t c) -> p t c", c=C)
        zT = shared[:, 2 * ST * C:2 * ST * C + 2 * SP_].rearrange("p (h q) -> p h q", h=2)
        hid = xT[:, 0:4 * SP_].rearrange("p (b q) -> p b q", b=2)
        mlp = xT[:, 4 * SP_:6 * SP_]
        x1c = t5T[:, :].rearrange("p (k q) -> p k q", k=NK)
        g_col, b_col, b2_col, ls_col, lsb2_col = (vecs[:, i:i + 1] for i in range(5))
        b1_cols = vecs[:, 5:5 + NJ]
        dws = t5[:, 0:K * K]
        spread = t5[:, 64:64 + RL]
        w8s = t5[0:C // 2, 1000:1000 + TAPS_W]
        w10s = xT[0:C // 2, 0:TAPS_H * P].rearrange("c (k o) -> c k o", k=TAPS_H)
        wc_sb = t5[:, 1100:1100 + NTAP]
        zero_frame = t5[0:T1H, 1200:1200 + T1W]

        consts_loaded = sem("consts_loaded")
        prep = sem("prep")
        prep_pe = sem("prep_pe")
        half_ready = sem("half_ready")
        frame_stored, rvec_stored = sem("frame_stored"), sem("rvec_stored")
        x_loaded = sem("x_loaded")
        st1_part, st1_ready = sem("st1_part"), sem("st1_ready")
        st2_part, st2_ready = sem("st2_part"), sem("st2_ready")
        gn_sems = {t: [sem(f"gn{t}_{s}") for s in ("mean", "neg", "dev", "dev_ready", "var", "var_eps", "rstd", "ready")] for t in (1, 2)}
        xn_ready = sem("xn_ready")
        min_done, t5_ready = sem("min_done"), sem("t5_ready")
        xT_psum, xT_ready = sem("xT_psum"), sem("xT_ready")
        t1_ready, t1T_psum, t1row_ready = sem("t1_ready"), sem("t1T_psum"), sem("t1row_ready")
        t1_stored, taps_loaded = sem("t1_stored"), sem("taps_loaded")
        t5T_psum, t5T_ready = sem("t5T_psum"), sem("t5T_ready")
        t11_psum, t12_ready = sem("t11_psum"), sem("t12_ready")
        m_psum, m_ready = sem("m_psum"), sem("m_ready")
        g_psum, gs_ready, g_ready = sem("g_psum"), sem("gs_ready"), sem("g_ready")
        kept_ready = sem("kept_ready")
        cst_psum, cst_ready = sem("cst_psum"), sem("cst_ready")
        x1_psum, x1_ready = sem("x1_psum"), sem("x1_ready")
        x1_stored = sem("x1_stored")
        xpad_ready = sem("xpad_ready")
        tile_psum, tile_ready = sem("tile_psum"), sem("tile_ready")
        toep_loaded = [sem("toep_loaded0"), sem("toep_loaded1")]
        conv_psum = sem("conv_psum")
        even_free, odd_free = sem("even_free"), sem("odd_free")
        ln_part, ln_aggr, ln_var_eps, ln_rstd, ln_ready = sem("ln_part"), sem("ln_aggr"), sem("ln_var_eps"), sem("ln_rstd"), sem("ln_ready")
        normed_ready, z_psum, z_ready = sem("normed_ready"), sem("z_psum"), sem("z_ready")
        h_psum, h_ready = sem("h_psum"), sem("h_ready")
        y_psum, y_ready = sem("y_psum"), sem("y_ready")
        x1c_loaded = [sem(f"x1c_loaded{k}") for k in range(NK)]
        sum_ready = sem("sum_ready")
        out_stored = [sem(f"out_stored{k}") for k in range(NK)]

        E = mybir.EngineType
        passed = {e: sem(f"passed_{n}") for e, n in ((E.SP, "sync"), (E.PE, "tensor"), (E.Activation, "scalar"), (E.DVE, "vector"))}

        N_CONST = 15
        block = ctx.enter_context(nc.Block())

        def wait_apart(eng, *waits):
            for s, count in waits:
                eng.wait_ge(s, count)
            eng.sem_inc(passed[eng.engine], 1)

        def slot(n):
            return (n % XS) * HW

        @block.sync
        def _(sp):
            def const(dst, src):
                sp.dma_start(dst, src).then_inc(consts_loaded, 16)

            sp.dma_start(xin[:, 0:HW], x[0]).then_inc(x_loaded, 16)
            const(dws, dw_rev)
            const(w8s, w8)
            const(w10s, w10t)
            const(ident[:, :], ident_in)
            const(gmat[:, :], gmat_in)
            const(w6s[:, :], w6t)
            const(p5[:, :], p5_w)
            const(w1s[:, :], w1t)
            const(w2s[:, :, :], w2t.rearrange("(j p) c -> p j c", p=P))
            const(dwb[:, :], bass.AP(dw_b.tensor, 0, [[0, TP], [1, C]]))
            const(g_col, ln_g)
            const(b_col, ln_b)
            const(b2_col, b2)
            const(ls_col, ls)
            const(b1_cols, b1)
            for n in range(1, XS):
                sp.wait_ge(x_loaded, 16 * n)
                sp.dma_start(xin[:, n * HW:(n + 1) * HW], x[n]).then_inc(x_loaded, 16)

            def load_x(n):
                sp.wait_ge(x_loaded, 16 * n)
                sp.dma_start(xin[:, bass.ds(slot(n), HW)], x[bass.ds(n % N, 1)].rearrange("a p q -> p (a q)")).then_inc(x_loaded, 16)

            def t1_round_trip(n):
                sp.wait_ge(t1row_ready, n + 1)
                for b, q, rows, cols in PIECES:
                    row, col = divmod(P * b + q, W)
                    sp.dma_start(bass.AP(t1pad, (2 + row) * T1W + 6 + col, [[CHR * T1W, NCH], [T1W, rows], [1, cols]]),
                                 t1row[NCH * b:NCH * (b + 1), q:q + rows * cols].rearrange("a (r w) -> a r w", w=cols)).then_inc(t1_stored, 16)
                sp.wait_ge(t1_stored, 16 * len(PIECES) * (n + 1))
                for k in range(TAPS_H):
                    sp.dma_start(taps[TAPS_W * k:TAPS_W * (k + 1)].rearrange("t (h w) -> t h w", w=W),
                                 bass.AP(t1pad, 2 * k * T1W, [[3, TAPS_W], [T1W, H], [1, W]])).then_inc(taps_loaded, 16)

            def store_x1(n):
                sp.wait_ge(x1_ready, NCH * n + NCH)
                sp.dma_start(x1_dram[bass.ds(n, 1)].rearrange("a p q -> p (a q)"), xin[:, bass.ds(slot(n), HW)]).then_inc(x1_stored, 16)

            def load_toeplitz(it, g, h):
                src = bass.AP(rvec, (it * UC + h * QC) * RL + 1, [[1, TP], [RL, QC], [1, TB]])
                sp.dma_start(shared[0:TP, h * QC * TB:(h + 1) * QC * TB].rearrange("p (c j) -> p c j", c=QC), src).then_inc(toep_loaded[h], 16)

            with sp.Fori(0, NG) as g:
                def turn(n):
                    t1_round_trip(n)
                    free_slot(n - 1)
                    load_x(n + 2)
                    store_x1(n)

                def free_slot(n):
                    sp.wait_ge(x1_stored, 16 * n + 16)
                    sp.wait_ge(xpad_ready, 2 * n + 2)

                t1_round_trip(g * GI)
                store_x1(g * GI)
                with sp.Fori(1, GI - 2) as i:
                    turn(g * GI + i)
                for n in (g * GI + GI - 2, g * GI + GI - 1):
                    t1_round_trip(n)
                    with sp.If(g < NG - 1):
                        free_slot(n - 1)
                        load_x(n + 2)
                    store_x1(n)
                with sp.If(g < NG - 1):
                    free_slot(g * GI + GI - 1)
                    load_x(g * GI + GI + 2)
                sp.wait_ge(t11_psum, NCH * GI * (g + 1))
                sp.wait_ge(rvec_stored, 16)
                for h in range(2):
                    load_toeplitz(0, g, h)
                with sp.Fori(1, C // UC) as it:
                    for h in range(2):
                        sp.wait_ge(conv_psum, g * C + (it - 1) * UC + (h + 1) * QC)
                        load_toeplitz(it, g, h)
                sp.wait_ge(x1_stored, 16 * GI * (g + 1))

                def load_x1c(n, k):
                    sp.dma_start(x1c[:, k, :], x1_dram[bass.ds(n, 1), :, 2 * SP_ * k:2 * SP_ * (k + 1)].rearrange("a p q -> p (a q)")).then_inc(x1c_loaded[k], 16)

                def store_out(n, k):
                    sp.wait_ge(sum_ready, NK * n + k + 1)
                    sp.dma_start(out[bass.ds(n, 1), :, 2 * SP_ * k:2 * SP_ * (k + 1)].rearrange("a p q -> p (a q)"), x1c[:, k, :]).then_inc(out_stored[k], 16)

                for k in range(NK):
                    load_x1c(g * GI, k)
                with sp.Fori(0, GI - 1) as i:
                    for k in range(NK):
                        store_out(g * GI + i, k)
                        sp.wait_ge(out_stored[k], 16 * (g * GI + i) + 16)
                        load_x1c(g * GI + i + 1, k)
                for k in range(NK):
                    store_out(g * GI + GI - 1, k)
                wait_apart(sp, *((out_stored[k], 16 * GI * (g + 1)) for k in range(NK)))

        @block.tensor
        def _(pe):
            mm = nc.tensor.matmul
            pe.wait_ge(consts_loaded, 16 * N_CONST)
            for k in range(TAPS_H):
                last = mm(ps[:, 7, TAPS_W * k:TAPS_W * (k + 1)], w10s[:, k, :], w8s, start=True, stop=True)
            last.then_inc(prep_pe, 1)
            pe.wait_ge(prep, 5)
            nc.tensor.transpose(ps[0:NTAP, 6, 0:P], wc_sb, ident[:, :]).then_inc(prep_pe, 1)
            pe.wait_ge(prep, 6)

            def gn_mean(t, n):
                st = gn1 if t == 1 else gn2
                pe.wait_ge(st1_ready if t == 1 else st2_ready, n + 1)
                mm(ps[:, 7, 0:1], gmat[:, :], st[:, 0:1], start=True, stop=True).then_inc(gn_sems[t][0], 1)

            def gn_var(t, n):
                st = gn1 if t == 1 else gn2
                pe.wait_ge(gn_sems[t][3], n + 1)
                mm(ps[:, 7, 0:1], gmat[:, :], st[:, 4:5], start=True, stop=True).then_inc(gn_sems[t][4], 1)

            def gn_used(t, n):
                pe.wait_ge(gn_sems[t][5], n + 1)

            def xT_chunks(n, ks):
                for k in ks:
                    if k in (0, NCH // 2):
                        pe.wait_ge(xn_ready, 2 * n + (1 if k == 0 else 2))
                    if k >= 2:
                        pe.wait_ge(xT_ready, NCH * n + k - 1)
                    for j in range(3):
                        q = (3 * k + j) * P
                        last = nc.tensor.transpose(ps[:, k % 2, j * P:(j + 1) * P], xn[:, q:q + P], ident[:, :])
                    last.then_inc(xT_psum, 1)

            def t1T(n):
                pe.wait_ge(t1_ready, n + 1)
                nc.tensor.transpose(ps[0:NT, 7, 0:P], t1[:, :], ident[:, :]).then_inc(t1T_psum, 1)

            def t5T_chunk(n, k):
                if k == 0:
                    pe.wait_ge(t5_ready, n + 1)
                else:
                    if k >= 2:
                        pe.wait_ge(t5T_ready, NCH * n + k - 1)
                for j in range(3):
                    q = (3 * k + j) * P
                    last = nc.tensor.transpose(ps[:, 2 + k % 2, j * P:(j + 1) * P], t5[:, q:q + P], ident[:, :])
                last.then_inc(t5T_psum, 1)

            def t11_chunk(n, k):
                if k == 0:
                    pe.wait_ge(taps_loaded, 16 * TAPS_H * (n + 1))
                else:
                    if k >= 2:
                        pe.wait_ge(t12_ready, NCH * n + k - 1)
                for j in range(3):
                    q = (3 * k + j) * P
                    last = mm(ps[:, 4 + k % 2, j * P:(j + 1) * P], taps[:, q:q + P], wcT[:, :], start=True, stop=True)
                last.then_inc(t11_psum, 1)

            def m_chunk(n, k):
                pe.wait_ge(t5T_ready, NCH * n + k + 1)
                pe.wait_ge(t12_ready, NCH * n + k + 1)
                for j in range(3):
                    q = (3 * k + j) * P
                    last = mm(ps[:, 6, 0:P], t5T[:, q:q + P], xT[:, q:q + P], start=(k == 0 and j == 0), stop=(k == NCH - 1 and j == 2))
                if k == NCH - 1:
                    last.then_inc(m_psum, 1)

            def x1_chunk(n, k):
                if k == 0:
                    pe.wait_ge(g_ready, n + 1)
                    pe.wait_ge(t5T_ready, NCH * n + NCH)
                if k >= 2:
                    pe.wait_ge(x1_ready, NCH * n + k - 1)
                mm(ps[:, 2 + k % 2, 0:CH], gi_sb[:, :], xin[:, bass.ds(slot(n) + k * CH, CH)], start=True, stop=True).then_inc(x1_psum, 1)

            def tile_chunk(n, k):
                if k in (0, NCH // 2):
                    pe.wait_ge(xpad_ready, 2 * n + (1 if k == 0 else 2))
                if k >= 2:
                    pe.wait_ge(tile_ready, NCH * n + k - 1)
                for j in range(4):
                    t = 4 * k + j
                    r = TR * (TH - 1 - t % TH)
                    src = xpad[:, t // TH, r:r + TR, :].rearrange("p r w -> p (r w)")
                    last = nc.tensor.transpose(ps[0:TP, 4 + k % 2, j * P:(j + 1) * P], src, ident[:, :])
                last.then_inc(tile_psum, 1)

            def layer0(n, prev, nxt):
                t1T(n)
                for k in range(NCH):
                    t5T_chunk(n, k)
                if prev:
                    pe.wait_ge(t1row_ready, n + 1)
                    gn_mean(2, n - 1)
                    gn_var(2, n - 1)
                    gn_used(2, n - 1)
                    for k in range(NCH):
                        tile_chunk(n - 1, k)
                else:
                    pe.wait_ge(t1row_ready, n + 1)
                if nxt:
                    gn_mean(1, n + 1)
                    gn_var(1, n + 1)
                    gn_used(1, n + 1)
                if prev:
                    pe.wait_ge(tile_ready, NCH * n)
                for k in range(NCH):
                    t11_chunk(n, k)
                    if k:
                        m_chunk(n, k - 1)
                m_chunk(n, NCH - 1)
                if nxt:
                    xT_chunks(n + 1, range(0, 3))
                pe.wait_ge(m_ready, n + 1)
                mm(ps[:, 6, 0:P], w6s[:, :], m_sb[:, :], start=True, stop=True).then_inc(g_psum, 1)
                if nxt:
                    xT_chunks(n + 1, range(3, 6))
                pe.wait_ge(gs_ready, n + 1)
                mm(ps[:, 7, 0:1], g_sb[:, :], kept[:, 1:2], start=True, stop=True).then_inc(cst_psum, 1)
                for k in range(NCH):
                    x1_chunk(n, k)
                wait_apart(pe, (cst_ready, n + 1), (x1_ready, NCH * n + NCH))

            with pe.Fori(0, NG) as g:
                n0 = g * GI
                gn_mean(1, n0)
                gn_var(1, n0)
                gn_used(1, n0)
                xT_chunks(n0, range(NCH))
                layer0(n0, False, True)
                with pe.Fori(1, GI - 1) as i:
                    layer0(n0 + i, True, True)
                layer0(n0 + GI - 1, True, False)
                gn_mean(2, n0 + GI - 1)
                gn_var(2, n0 + GI - 1)
                gn_used(2, n0 + GI - 1)
                for k in range(NCH):
                    tile_chunk(n0 + GI - 1, k)
                wait_apart(pe, (tile_ready, NCH * (n0 + GI)))

                with pe.Fori(0, C // UC) as it:
                    for u in range(UC):
                        if u % QC == 0:
                            pe.wait_ge(toep_loaded[u // QC], 16 * (g * (C // UC) + it) + 16)
                        pe.wait_ge((even_free, odd_free)[u % 2], (g * (C // UC) + it) * (UC // 2) + u // 2 + 1)
                        T = shared[0:TP, u * TB:(u + 1) * TB]
                        o = ps[0:TP, u, 0:TG].rearrange("p (s t) -> p s t", t=TH)
                        r = tiles[:, bass.ds(it * UC + u, 1), :].rearrange("p a (s t) -> p (a s) t", t=TH)
                        mm(o, T[:, TP:2 * TP], r, start=True, stop=False)
                        mm(o[:, :, 0:TH - 1], T[:, 0:TP], r[:, :, 1:TH], start=False, stop=False)
                        mm(o[:, :, 1:TH], T[:, 2 * TP:3 * TP], r[:, :, 0:TH - 1], start=False, stop=True).then_inc(conv_psum, 1)
                wait_apart(pe, (even_free, (g + 1) * (C // 2) + UC // 2), (odd_free, (g + 1) * (C // 2) + UC // 2))

                def z_tiles(s):
                    pe.wait_ge(normed_ready, s + 1)
                    for h in range(2):
                        for t in range(ST):
                            last = nc.tensor.transpose(ps[:, h, t * TP:(t + 1) * TP], normed[:, h * ST + t, :], ident[0:TP, 0:TP])
                    last.then_inc(z_psum, 1)

                def up(s, j):
                    if j == 0:
                        pe.wait_ge(z_ready, s + 1)
                    if j >= 2:
                        pe.wait_ge(h_ready, NJ * s + j - 1)
                    for h in range(2):
                        last = mm(ps[:, 2 + 2 * (j % 2) + h, 0:SP_], w1s[:, j * P:(j + 1) * P], zT[:, h, :], start=True, stop=True)
                    last.then_inc(h_psum, 1)

                def down(s, j):
                    pe.wait_ge(h_ready, NJ * s + j + 1)
                    for h in range(2):
                        last = mm(ps[:, 6 + h, 0:SP_], w2s[:, j, :], hid[:, j % 2, h * SP_:(h + 1) * SP_], start=(j == 0), stop=(j == NJ - 1))
                    if j == NJ - 1:
                        last.then_inc(y_psum, 1)

                def step(s, more):
                    up(s, 0)
                    up(s, 1)
                    pe.wait_ge(y_ready, s)
                    down(s, 0)
                    up(s, 2)
                    down(s, 1)
                    up(s, 3)
                    if more:
                        z_tiles(s + 1)
                    down(s, 2)
                    down(s, 3)

                z_tiles(NK * n0)
                with pe.Fori(0, GI - 1) as i:
                    for k in range(NK):
                        step(NK * (n0 + i) + k, True)
                for k in range(NK):
                    step(NK * (n0 + GI - 1) + k, k < NK - 1)
                pe.wait_ge(y_ready, NK * (n0 + GI))

        @block.gpsimd
        def _(pool):
            pool.wait_ge(prep, 4)
            pool.dma_start(bass.AP(rvec, 0, [[RL, C], [1, RL]]), spread).then_inc(rvec_stored, 16)
            pool.dma_start(bass.AP(t1pad, 0, [[T1W, T1H], [1, T1W]]), zero_frame).then_inc(frame_stored, 16)
            nc.gpsimd.memset(minus_half[:, :], -0.5).then_inc(half_ready, 1)
            pool.wait_ge(half_ready, 1)
            pool.wait_ge(consts_loaded, 16 * N_CONST)

            def gn_power(t, n):
                st = (gn1, gn2)[t - 1]
                pool.wait_ge(gn_sems[t][5], n + 1)
                nc.gpsimd.tensor_tensor(st[:, 5:6], st[:, 5:6], minus_half[:, 0:1], ALU.pow).then_inc(gn_sems[t][6], 1)

            def weigh(n):
                pool.wait_ge(min_done, n + 1)
                nc.gpsimd.tensor_tensor(t5[:, :], t5[:, :], p5[:, :], ALU.mult).then_inc(t5_ready, 1)

            def ln_power(s):
                pool.wait_ge(ln_var_eps, s + 1)
                nc.gpsimd.tensor_tensor(lnr[:, 0, :], lnr[:, 0, :], minus_half[0:TP, :], ALU.pow).then_inc(ln_rstd, 1)

            def residual(n, s, k):
                pool.wait_ge(x1c_loaded[k], 16 * n + 16)
                pool.wait_ge(y_ready, s + 1)
                xk = x1c[:, k, :].rearrange("p (r h w) -> p h r w", h=2, w=HALF)
                nc.gpsimd.tensor_tensor(xk, xk, mlp.rearrange("p (h r w) -> p h r w", h=2, w=HALF), ALU.add).then_inc(sum_ready, 1)

            with pool.Fori(0, NG) as g:
                n0 = g * GI
                gn_power(1, n0)
                weigh(n0)
                gn_power(1, n0 + 1)
                weigh(n0 + 1)
                with pool.Fori(1, GI - 1) as i:
                    gn_power(2, n0 + i - 1)
                    gn_power(1, n0 + i + 1)
                    weigh(n0 + i + 1)
                gn_power(2, n0 + GI - 2)
                gn_power(2, n0 + GI - 1)
                ln_power(NK * n0)
                with pool.Fori(0, GI - 1) as i:
                    for k in range(NK):
                        ln_power(NK * (n0 + i) + k + 1)
                        residual(n0 + i, NK * (n0 + i) + k, k)
                for k in range(NK):
                    if k < NK - 1:
                        ln_power(NK * (n0 + GI - 1) + k + 1)
                    residual(n0 + GI - 1, NK * (n0 + GI - 1) + k, k)

        @block.scalar
        def _(act):
            def copy(out_, in_):
                return nc.scalar.activation(out_, in_, ACT.Identity)

            def normalise(n):
                wait_apart(act, (gn_sems[1][7], n + 1), (min_done, n))
                for h in range(2):
                    q = h * (HW // 2)
                    nc.scalar.activation(xn[:, q:q + HW // 2], xin[:, bass.ds(slot(n) + q, HW // 2)], ACT.Identity,
                                         scale=gn1[:, 5:6], bias=gn1[:, 6:7]).then_inc(xn_ready, 1)

            def xT_copies(n, ks):
                for k in ks:
                    act.wait_ge(xT_psum, NCH * n + k + 1)
                    copy(xT[:, k * CH:(k + 1) * CH], ps[:, k % 2, 0:CH]).then_inc(xT_ready, 1)

            def backwards(h, c):
                full = xpad[:, h, :, :]
                last = (H - 1) * PW + PW - 1 - c
                return bass.AP(full.tensor, full.offset + last, [full.ap[0], [-PW, H], [-1, PW - HALO]])

            def pad(n):
                wait_apart(act, (gn_sems[2][7], n + 1), (tile_psum, NCH * n))
                v = xin[:, bass.ds(slot(n), HW)].rearrange("p (r w) -> p r w", w=W)
                nc.scalar.activation(backwards(0, HALO), v[:, :, 0:PW - HALO], ACT.Identity,
                                     scale=gn2[:, 5:6], bias=gn2[:, 6:7]).then_inc(xpad_ready, 1)
                nc.scalar.activation(backwards(1, 0), v[:, :, HALF - HALO:W], ACT.Identity,
                                     scale=gn2[:, 5:6], bias=gn2[:, 6:7]).then_inc(xpad_ready, 1)

            def tile_copies(n, i):
                for k in range(NCH):
                    wait_apart(act, (tile_psum, NCH * n + k + 1))
                    dst = tiles[:, :, bass.ds(i * TI + 4 * k, 4)].rearrange("p c t -> p t c")
                    copy(dst, ps[0:TP, 4 + k % 2, 0:4 * P].rearrange("p (t c) -> p t c", c=C)).then_inc(tile_ready, 1)

            def layer0(n, i, prev, nxt):
                if not prev:
                    for k in range(NK):
                        act.wait_ge(out_stored[k], 16 * n)
                for k in range(NCH):
                    act.wait_ge(t5T_psum, NCH * n + k + 1)
                    copy(t5T[:, k * CH:(k + 1) * CH], ps[:, 2 + k % 2, 0:CH]).then_inc(t5T_ready, 1)
                if prev:
                    pad(n - 1)
                    tile_copies(n - 1, i - 1)
                if nxt:
                    normalise(n + 1)
                    act.wait_ge(m_psum, n + 1)
                    xT_copies(n + 1, range(NCH))
                for k in range(NCH):
                    if k == 0:
                        wait_apart(act, (x1_psum, NCH * n + 1), (cst_ready, n + 1))
                    else:
                        wait_apart(act, (x1_psum, NCH * n + k + 1))
                    nc.scalar.activation(xin[:, bass.ds(slot(n) + k * CH, CH)], ps[:, 2 + k % 2, 0:CH], ACT.Identity,
                                         bias=cst[:, :]).then_inc(x1_ready, 1)

            act.wait_ge(consts_loaded, 16 * N_CONST)
            with act.Fori(0, NG) as g:
                n0 = g * GI
                normalise(n0)
                act.wait_ge(sum_ready, NK * n0)
                xT_copies(n0, range(NCH))
                layer0(n0, 0, False, True)
                with act.Fori(1, GI - 1) as i:
                    layer0(n0 + i, i, True, True)
                layer0(n0 + GI - 1, GI - 1, True, False)
                pad(n0 + GI - 1)
                tile_copies(n0 + GI - 1, GI - 1)

                with act.Fori(0, C // UC) as it:
                    for u in range(0, UC, 2):
                        wait_apart(act, (conv_psum, g * C + it * UC + u + 1))
                        nc.scalar.activation(tiles[:, bass.ds(it * UC + u, 1), :].rearrange("p a t -> p (a t)"), ps[0:TP, u, 0:TG],
                                             ACT.Identity, bias=dwb[:, bass.ds(it * UC + u, 1)]).then_inc(even_free, 1)

                def step(s):
                    for j in range(NJ):
                        act.wait_ge(h_psum, NJ * s + j + 1)
                        nc.scalar.activation(hid[:, j % 2, :].rearrange("p (h q) -> p h q", h=2), ps[:, 2 + 2 * (j % 2):4 + 2 * (j % 2), 0:SP_],
                                             ACT.Gelu_apprx_tanh, bias=b1_cols[:, j:j + 1]).then_inc(h_ready, 1)
                    act.wait_ge(y_psum, s + 1)
                    act.wait_ge(sum_ready, s)
                    nc.scalar.activation(mlp.rearrange("p (h q) -> p h q", h=2), ps[:, 6:8, 0:SP_], ACT.Identity,
                                         scale=ls_col, bias=lsb2_col).then_inc(y_ready, 1)

                with act.Fori(0, GI) as i:
                    for k in range(NK):
                        step(NK * (n0 + i) + k)

        @block.vector
        def _(dve):
            v = nc.vector
            v.memset(spread, 0.0).then_inc(prep, 1)
            v.memset(zero_frame, 0.0).then_inc(prep, 1)
            v.memset(xpad[:, :, :, :], 0.0).then_inc(prep, 1)
            dve.sem_inc(even_free, UC // 2)
            dve.sem_inc(odd_free, UC // 2)
            dve.wait_ge(consts_loaded, 16 * N_CONST)
            dve.wait_ge(prep, 3)
            first = 2 * TP - KC * PW - KC
            v.tensor_copy(spread[:, first:first + K * PW].rearrange("p (y x) -> p y x", x=PW)[:, :, 0:K],
                          dws.rearrange("p (y x) -> p y x", x=K)).then_inc(prep, 1)
            dve.wait_ge(prep_pe, 1)
            v.tensor_copy(wc_sb, ps[:, 7, 0:NTAP]).then_inc(prep, 1)
            dve.wait_ge(prep_pe, 2)
            v.tensor_copy(wcT[:, 1:P], ps[0:NTAP, 6, 0:P - 1])
            v.tensor_copy(wcT[:, 0:1], ps[0:NTAP, 6, P - 1:P]).then_inc(prep, 1)
            v.tensor_tensor(lsb2_col, ls_col, b2_col, ALU.mult).then_inc(prep, 1)
            dve.wait_ge(frame_stored, 16)
            dve.wait_ge(rvec_stored, 16)

            def moments(t, n, k, base):
                (s, part) = ((st1, st1_part), (st2, st2_part))[t - 1]
                v.bn_stats(s[:, k, :], xin[:, bass.ds(slot(n) + k * CH, CH)]).then_inc(part, 1)

            def aggregate(t, n):
                (s, part, st, ready) = ((st1, st1_part, gn1, st1_ready), (st2, st2_part, gn2, st2_ready))[t - 1]
                wait_apart(dve, (part, NCH * (n + 1)))
                v.bn_aggr(st[:, 0:2], s[:, :, :]).then_inc(ready, 1)

            def gn_chain(t, n):
                st = (gn1, gn2)[t - 1]
                s_mean, s_neg, s_dev, s_dev_ready, s_var, s_var_eps, s_rstd, s_ready = gn_sems[t]
                dve.wait_ge(s_mean, n + 1)
                v.tensor_scalar(st[:, 2:3], ps[:, 7, 0:1], -1.0, None, ALU.mult).then_inc(s_neg, 1)
                dve.wait_ge(s_neg, n + 1)
                v.tensor_tensor(st[:, 3:4], st[:, 0:1], st[:, 2:3], ALU.add).then_inc(s_dev, 1)
                dve.wait_ge(s_dev, n + 1)
                v.scalar_tensor_tensor(out=st[:, 4:5], in0=st[:, 3:4], scalar=st[:, 3:4], in1=st[:, 1:2],
                                       op0=ALU.mult, op1=ALU.add).then_inc(s_dev_ready, 1)
                dve.wait_ge(s_var, n + 1)
                v.tensor_scalar(st[:, 5:6], ps[:, 7, 0:1], GN_EPS, None, ALU.add).then_inc(s_var_eps, 1)
                dve.wait_ge(s_rstd, n + 1)
                v.tensor_tensor(st[:, 6:7], st[:, 2:3], st[:, 5:6], ALU.mult).then_inc(s_ready, 1)

            def stats_x(n):
                wait_apart(dve, (x_loaded, 16 * n + 16))
                for k in range(NCH):
                    moments(1, n, k, None)
                aggregate(1, n)
                gn_chain(1, n)

            def shifted_min(n):
                dve.wait_ge(xn_ready, 2 * n + 2)
                a = xn[:, :].rearrange("p (r w) -> p r w", w=W)
                o = t5[:, :].rearrange("p (r w) -> p r w", w=W)
                v.tensor_tensor(o[:, :, 1:W], a[:, :, 1:W], a[:, :, 0:W - 1], ALU.min)
                v.tensor_tensor(o[:, :, 0:1], a[:, :, 0:1], a[:, :, W - 1:W], ALU.min).then_inc(min_done, 1)

            def channel_max(n):
                for h in range(2):
                    dve.wait_ge(xT_ready, NCH * n + 3 * (h + 1))
                    last = v.tensor_reduce(t1[:, :].rearrange("p (b a) -> p a b", b=NB)[:, 3 * h:3 * h + 3, :],
                                           xT[:, 9 * P * h:9 * P * (h + 1)].rearrange("p (a b c) -> p a b c", b=NB, c=P), AX_X, ALU.max)
                last.then_inc(t1_ready, 1)

            def layer0(n, prev, nxt):
                dve.wait_ge(t1T_psum, n + 1)
                v.tensor_copy(t1row[:, :], ps[0:NT, 7, 0:P]).then_inc(t1row_ready, 1)
                v.tensor_copy(kept[:, :], gn1[:, 5:7]).then_inc(kept_ready, 1)
                if prev:
                    gn_chain(2, n - 1)
                if nxt:
                    stats_x(n + 1)
                for k in range(NCH):
                    dve.wait_ge(t11_psum, NCH * n + k + 1)
                    q = k * CH
                    v.tensor_tensor(xT[:, q:q + CH], xT[:, q:q + CH], ps[:, 4 + k % 2, 0:CH], ALU.max).then_inc(t12_ready, 1)
                dve.wait_ge(m_psum, n + 1)
                v.tensor_copy(m_sb[:, :], ps[:, 6, 0:P]).then_inc(m_ready, 1)
                dve.wait_ge(g_psum, n + 1)
                v.tensor_scalar(g_sb[:, :], ps[:, 6, 0:P], SCALE, None, ALU.mult).then_inc(gs_ready, 1)
                dve.wait_ge(gs_ready, n + 1)
                dve.wait_ge(kept_ready, n + 1)
                v.scalar_tensor_tensor(out=gi_sb[:, :], in0=g_sb[:, :], scalar=kept[:, 0:1], in1=ident[:, :],
                                       op0=ALU.mult, op1=ALU.add).then_inc(g_ready, 1)
                dve.wait_ge(cst_psum, n + 1)
                v.tensor_copy(cst[:, :], ps[:, 7, 0:1]).then_inc(cst_ready, 1)
                if nxt:
                    shifted_min(n + 1)
                    channel_max(n + 1)
                for k in range(NCH):
                    wait_apart(dve, (x1_ready, NCH * n + k + 1))
                    moments(2, n, k, None)
                aggregate(2, n)

            with dve.Fori(0, NG) as g:
                n0 = g * GI
                stats_x(n0)
                shifted_min(n0)
                channel_max(n0)
                layer0(n0, False, True)
                with dve.Fori(1, GI - 1) as i:
                    layer0(n0 + i, True, True)
                layer0(n0 + GI - 1, True, False)
                gn_chain(2, n0 + GI - 1)

                with dve.Fori(0, C // UC) as it:
                    for u in range(1, UC, 2):
                        dve.wait_ge(conv_psum, g * C + it * UC + u + 1)
                        v.tensor_scalar(tiles[:, bass.ds(it * UC + u, 1), :].rearrange("p a t -> p (a t)"), ps[0:TP, u, 0:TG],
                                        dwb[:, bass.ds(it * UC + u, 1)], None, ALU.add).then_inc(odd_free, 1)
                wait_apart(dve, (even_free, (g + 1) * (C // 2) + UC // 2), (odd_free, (g + 1) * (C // 2) + UC // 2))

                def step(i, s, k):
                    idx = [(h * ST + t, i * TI + h * TH + ST * k + t) for h in range(2) for t in range(ST)]

                    def tile(m):
                        return tiles[:, :, bass.ds(m, 1)].rearrange("p c a -> p (c a)")

                    for j, m in idx:
                        last = v.bn_stats(lnst[:, j, :], tile(m))
                    last.then_inc(ln_part, 1)
                    wait_apart(dve, (ln_part, s + 1))
                    for j, m in idx:
                        last = v.bn_aggr(lnmv[:, j, :], lnst[:, j, :])
                    last.then_inc(ln_aggr, 1)
                    dve.wait_ge(ln_aggr, s + 1)
                    v.tensor_scalar(lnr[:, 0, :], lnmv[:, :, 1], LN_EPS, None, ALU.add).then_inc(ln_var_eps, 1)
                    dve.wait_ge(ln_rstd, s + 1)
                    v.scalar_tensor_tensor(out=lnr[:, 1, :], in0=lnmv[:, :, 0], scalar=-1.0, in1=lnr[:, 0, :],
                                           op0=ALU.mult, op1=ALU.mult).then_inc(ln_ready, 1)
                    dve.wait_ge(ln_ready, s + 1)
                    dve.wait_ge(z_psum, s)
                    for j, m in idx:
                        last = v.tensor_scalar(normed[:, j, :], tile(m), lnr[:, 0, j:j + 1], lnr[:, 1, j:j + 1], ALU.mult, ALU.add)
                    last.then_inc(normed_ready, 1)
                    dve.wait_ge(z_psum, s + 1)
                    for h in range(2):
                        last = v.tensor_scalar(zT[:, h, :].rearrange("p (r w) -> p r w", w=HALF),
                                               ps[:, h, 0:ST * TP].rearrange("p (r w) -> p r w", w=PW)[:, :, HALO:HALO + HALF],
                                               g_col, b_col, ALU.mult, ALU.add)
                    last.then_inc(z_ready, 1)

                with dve.Fori(0, GI) as i:
                    for k in range(NK):
                        step(i, NK * (n0 + i) + k, k)


_INS = ["x", "p5_w", "w6t", "w8", "w10t", "dw_rev", "dw_b", "ln_g", "ln_b", "w1t", "b1", "w2t", "b2", "ls", "ident", "gmat"]


def kernel(**inputs):
    import numpy as np
    import concourse.bacc as bacc
    from concourse.bass_utils import run_bass_kernel_spmd

    a = {k: np.asarray(v) for k, v in inputs.items()}
    N, C, H, W = a["x"].shape
    col = lambda v: v.reshape(-1, 1)
    arrays = {
        "x": a["x"].reshape(N, C, H * W),
        "p5_w": a["L0_conv_p5_w"].reshape(C, H * W),
        "w6t": a["L0_conv_w6"].T,
        "w8": a["L0_conv_w8"].reshape(C // 2, -1),
        "w10t": a["L0_conv_w10"].T.reshape(C // 2, 3, C),
        "dw_rev": a["L1_conv_dw_w"].reshape(C, -1)[:, ::-1],
        "dw_b": a["L1_conv_dw_b"],
        "ln_g": col(a["L1_conv_ln_g"]),
        "ln_b": col(a["L1_conv_ln_b"]),
        "w1t": a["L1_conv_w1"].T,
        "b1": a["L1_conv_b1"].reshape(-1, C).T,
        "w2t": a["L1_conv_w2"].T,
        "b2": col(a["L1_conv_b2"]),
        "ls": col(a["L1_conv_ls"]),
        "ident": np.eye(C, dtype=np.float32),
        "gmat": np.kron(np.eye(32, dtype=np.float32), np.full((C // 32, C // 32), 32 / C, np.float32)),
    }
    nc = bacc.Bacc("TRN2", target_bir_lowering=False, num_devices=1)
    named, args = {}, []
    for name in _INS:
        v = np.ascontiguousarray(arrays[name])
        named[f"in_{name}"] = v
        args.append(nc.dram_tensor(f"in_{name}", v.shape, mybir.dt.from_np(v.dtype), kind="ExternalInput").ap())
    out = nc.dram_tensor("out_0", (N, C, H * W), F32, kind="ExternalOutput").ap()
    build(nc, *args, out)
    r = run_bass_kernel_spmd(nc, [named], core_ids=[0])
    return r.results[0]["out_0"].reshape(N, C, H, W)
```

```python
from contextlib import ExitStack

import concourse.bass as bass
from concourse import mybir

F32 = mybir.dt.float32
BF16 = mybir.dt.bfloat16
ALU = mybir.AluOpType
ACT = mybir.ActivationFunctionType
AX_X = mybir.AxisListType.X


def build(nc, x, p5_w, w6t, w8, w10t, dw_rev, dw_b, ln_g, ln_b, w1t, b1, w2t, b2, ls, ident_in, gmat_in, edge_in, out):
    N, C, HW = x.shape
    W = H = 48
    P = 128
    GI = 8
    NG = N // GI
    XS = 3
    CH = 384
    NCH = HW // CH
    NT = HW // P
    NM = 3
    HID = w1t.shape[1]
    NJ = HID // P
    HALF, HALO = W // 2, 3
    PW = HALF + 2 * HALO
    TR = 4
    TP = TR * PW
    TH = H // TR
    TI = 2 * TH
    TG = GI * TI
    K = 7
    KC = K // 2
    TAPS_H, TAPS_W = 3, 5
    NTAP = TAPS_H * TAPS_W
    EDGE = 3 * (TAPS_W // 2)
    NS = 3
    SETS = (NS, NS, 2)
    NPL = sum(SETS)
    TROWS = NTAP * NPL
    NR = NT + 1
    RL = 4 * TP
    TB = 3 * TP
    QC = 4
    UC = 2 * QC
    NK = 3
    SR = H // NK
    ST = SR // TR
    SP_ = SR * HALF
    GN_EPS, LN_EPS = 1e-5, 1e-5
    SCALE = -1.0 / (float(C) ** 0.5 * float(HW) ** 0.5)
    assert PW * KC + KC <= TP and SP_ == CH and 2 * SP_ * NK == HW

    t1pad = nc.dram_tensor("t1pad", (1 + len(SETS) * NS * NR, P), BF16, kind="Internal")
    rvec = nc.dram_tensor("rvec", (C, RL), F32, kind="Internal")
    x1_dram = nc.dram_tensor("x1_dram", (N, C, HW), F32, kind="Internal").ap()

    with ExitStack() as ctx:
        def sb(name, shape, dtype=F32):
            return ctx.enter_context(nc.sbuf_tensor(name, shape, dtype))

        def sem(name):
            return ctx.enter_context(nc.semaphore(name))

        tiles = sb("tiles", [TP, C, TG])
        xin = sb("xin", [P, XS * HW])
        xn = sb("xn", [P, HW])
        t5 = sb("t5", [P, HW])
        p5 = sb("p5", [P, HW])
        xT = sb("xT", [P, HW])
        t5T = sb("t5T", [P, HW])
        xpad = sb("xpad", [P, 2, H, PW])
        shared = sb("shared", [P, UC * TB])
        ident = sb("ident", [P, P])
        gmat = sb("gmat", [P, P])
        w6s = sb("w6s", [P, P])
        wcT = sb("wcT", [TROWS, P], BF16)
        w1s = sb("w1s", [P, HID])
        w2s = sb("w2s", [P, NJ, P])
        dwb = sb("dwb", [TP, C])
        vecs = sb("vecs", [P, 12])
        m_sb = sb("m_sb", [P, P])
        g_sb = sb("g_sb", [P, P])
        gi_sb = sb("gi_sb", [P, P])
        t1 = sb("t1", [P, NT])
        t1s = sb("t1s", [P, NS, NR], BF16)
        t1rest = sb("t1rest", [P, NT])
        t1row = sb("t1row", [NS * NR, P], BF16)
        ident_b = sb("ident_b", [P, P], BF16)
        edge = sb("edge", [TROWS, 2 * EDGE])
        st1 = sb("st1", [P, NCH, 6])
        st2 = sb("st2", [P, NCH, 6])
        gn = sb("gn", [P, 2, 7])
        kept = sb("kept", [P, 2])
        cst = sb("cst", [P, 1])
        lnst = sb("lnst", [TP, 2 * ST, 6])
        lnmv = sb("lnmv", [TP, 2 * ST, 2])
        lnr = sb("lnr", [TP, 2, 2 * ST])
        minus_half = sb("minus_half", [P, 2 * ST])
        ps = ctx.enter_context(nc.psum_tensor("ps", [P, 8, 512], F32))

        taps = shared[0:TROWS, 0:HW // 2].bitcast(BF16)
        normed = shared[0:TP, 0:2 * ST * C].rearrange("p (t c) -> p t c", c=C)
        zT = shared[:, 2 * ST * C:2 * ST * C + 2 * SP_].rearrange("p (h q) -> p h q", h=2)
        hid = xT[:, 0:4 * SP_].rearrange("p (b q) -> p b q", b=2)
        mlp = xT[:, 4 * SP_:6 * SP_]
        x1c = t5T[:, :].rearrange("p (k q) -> p k q", k=NK)
        g_col, b_col, b2_col, ls_col, lsb2_col = (vecs[:, i:i + 1] for i in range(5))
        b1_cols = vecs[:, 5:5 + NJ]
        dws = t5[:, 0:K * K]
        spread = t5[:, 64:64 + RL]
        w8s = t5[0:C // 2, 1000:1000 + TAPS_W]
        w10s = xT[0:C // 2, 0:TAPS_H * P].rearrange("c (k o) -> c k o", k=TAPS_H)
        wc_sb = t5[:, 1100:1100 + NTAP]
        wc_part = t5[:, 1200:1200 + 24].bitcast(BF16).rearrange("o (s t) -> o s t", s=NS)
        wc_rest = t5[:, 1232:1232 + NTAP]
        wc_rows = t5[:, 1300:1300 + TROWS]
        zero_frame = t5[0:1 + NS * NR, 1500:1500 + P // 2].bitcast(BF16)

        consts_loaded = sem("consts_loaded")
        prep = sem("prep")
        prep_pe = sem("prep_pe")
        wc_split = sem("wc_split")
        half_ready = sem("half_ready")
        frame_stored, rvec_stored = sem("frame_stored"), sem("rvec_stored")
        x_loaded = sem("x_loaded")
        GN_STEPS = ("part", "stats", "mean", "neg", "dev", "square", "spread", "var", "var_eps", "rstd", "ready")
        gnx = {step: sem(f"gnx_{step}") for step in GN_STEPS}
        gn1 = {step: sem(f"gn1_{step}") for step in GN_STEPS}
        xn_ready = sem("xn_ready")
        min_done, t5_ready = sem("min_done"), sem("t5_ready")
        xT_psum, xT_ready = sem("xT_psum"), sem("xT_ready")
        t1_ready, t1T_psum, t1row_ready = sem("t1_ready"), sem("t1T_psum"), sem("t1row_ready")
        t1_whole, t1_high, t1_left = sem("t1_whole"), sem("t1_high"), sem("t1_left")
        t1_stored, taps_loaded = sem("t1_stored"), sem("taps_loaded")
        taps_ready = sem("taps_ready")
        t5T_psum, t5T_ready = sem("t5T_psum"), sem("t5T_ready")
        t11_psum, t12_ready = sem("t11_psum"), sem("t12_ready")
        m_psum, m_ready = sem("m_psum"), sem("m_ready")
        g_psum, gs_ready, g_ready = sem("g_psum"), sem("gs_ready"), sem("g_ready")
        kept_ready = sem("kept_ready")
        cst_psum, cst_ready = sem("cst_psum"), sem("cst_ready")
        x1_psum, x1_ready = sem("x1_psum"), sem("x1_ready")
        x1_stored = sem("x1_stored")
        xpad_ready = sem("xpad_ready")
        tile_psum, tile_ready = sem("tile_psum"), sem("tile_ready")
        toep_loaded = [sem("toep_loaded0"), sem("toep_loaded1")]
        conv_psum = sem("conv_psum")
        even_free, odd_free = sem("even_free"), sem("odd_free")
        ln_part, ln_aggr, ln_var_eps, ln_rstd, ln_ready = sem("ln_part"), sem("ln_aggr"), sem("ln_var_eps"), sem("ln_rstd"), sem("ln_ready")
        normed_ready, z_psum, z_ready = sem("normed_ready"), sem("z_psum"), sem("z_ready")
        h_psum, h_ready = sem("h_psum"), sem("h_ready")
        y_psum, y_ready = sem("y_psum"), sem("y_ready")
        x1c_loaded = [sem(f"x1c_loaded{k}") for k in range(NK)]
        sum_ready = sem("sum_ready")
        out_stored = [sem(f"out_stored{k}") for k in range(NK)]

        E = mybir.EngineType
        passed = {e: sem(f"passed_{n}") for e, n in ((E.SP, "sync"), (E.PE, "tensor"), (E.Activation, "scalar"), (E.DVE, "vector"))}

        N_CONST = 16
        block = ctx.enter_context(nc.Block())

        def wait_apart(eng, *waits):
            for s, count in waits:
                eng.wait_ge(s, count)
            eng.sem_inc(passed[eng.engine], 1)

        def tile_bank(k):
            return (4, 5, 2, 3)[k % 4]

        def x1_bank(k):
            return (2, 3, 0, 1)[k % 4]

        t5T_bank = x1_bank

        def slot(n):
            return (n % XS) * HW

        @block.sync
        def _(sp):
            def const(dst, src):
                sp.dma_start(dst, src).then_inc(consts_loaded, 16)

            sp.dma_start(xin[:, 0:HW], x[0]).then_inc(x_loaded, 16)
            const(dws, dw_rev)
            const(w8s, w8)
            const(w10s, w10t)
            const(ident[:, :], ident_in)
            const(gmat[:, :], gmat_in)
            const(edge[:, :], edge_in)
            const(w6s[:, :], w6t)
            const(p5[:, :], p5_w)
            const(w1s[:, :], w1t)
            const(w2s[:, :, :], w2t.rearrange("(j p) c -> p j c", p=P))
            const(dwb[:, :], bass.AP(dw_b.tensor, 0, [[0, TP], [1, C]]))
            const(g_col, ln_g)
            const(b_col, ln_b)
            const(b2_col, b2)
            const(ls_col, ls)
            const(b1_cols, b1)
            for n in range(1, XS):
                sp.wait_ge(x_loaded, 16 * n)
                sp.dma_start(xin[:, n * HW:(n + 1) * HW], x[n]).then_inc(x_loaded, 16)

            def load_x(n):
                sp.wait_ge(x_loaded, 16 * n)
                sp.dma_start(xin[:, bass.ds(slot(n), HW)], x[bass.ds(n % N, 1)].rearrange("a p q -> p (a q)")).then_inc(x_loaded, 16)

            def t1_round_trip(n):
                sp.wait_ge(t1row_ready, n + 1)
                sp.dma_start(bass.AP(t1pad, P, [[P, NS * NR], [NS * NR * P, len(SETS)], [1, P]]),
                             t1row[:, :].unsqueeze(1).to_broadcast([NS * NR, len(SETS), P])).then_inc(t1_stored, 16)
                sp.wait_ge(t1_stored, 16 * (n + 1))
                rows = NPL * TAPS_W
                for k in range(TAPS_H):
                    sp.dma_start(taps[k * rows:(k + 1) * rows],
                                 bass.AP(t1pad, P + (2 * k - 2) * W - EDGE, [[NR * P, NPL], [3, TAPS_W], [1, HW]])).then_inc(taps_loaded, 16)

            def store_x1(n):
                sp.wait_ge(x1_ready, NCH * n + NCH)
                sp.dma_start(x1_dram[bass.ds(n, 1)].rearrange("a p q -> p (a q)"), xin[:, bass.ds(slot(n), HW)]).then_inc(x1_stored, 16)

            def load_toeplitz(it, g, h):
                src = bass.AP(rvec, (it * UC + h * QC) * RL + 1, [[1, TP], [RL, QC], [1, TB]])
                sp.dma_start(shared[0:TP, h * QC * TB:(h + 1) * QC * TB].rearrange("p (c j) -> p c j", c=QC), src).then_inc(toep_loaded[h], 16)

            with sp.Fori(0, NG) as g:
                def free_slot(n):
                    sp.wait_ge(x1_stored, 16 * n + 16)
                    sp.wait_ge(xpad_ready, 2 * n + 2)

                t1_round_trip(g * GI)
                t1_round_trip(g * GI + 1)
                store_x1(g * GI)
                with sp.Fori(1, GI - 2) as i:
                    free_slot(g * GI + i - 1)
                    load_x(g * GI + i + 2)
                    t1_round_trip(g * GI + i + 1)
                    store_x1(g * GI + i)
                for i in (GI - 2, GI - 1):
                    n = g * GI + i
                    with sp.If(g < NG - 1):
                        free_slot(n - 1)
                        load_x(n + 2)
                    if i < GI - 1:
                        t1_round_trip(n + 1)
                    store_x1(n)
                with sp.If(g < NG - 1):
                    free_slot(g * GI + GI - 1)
                    load_x(g * GI + GI + 2)
                sp.wait_ge(t11_psum, NCH * GI * (g + 1))
                sp.wait_ge(rvec_stored, 16)
                for h in range(2):
                    load_toeplitz(0, g, h)
                with sp.Fori(1, C // UC) as it:
                    for h in range(2):
                        sp.wait_ge(conv_psum, g * C + (it - 1) * UC + (h + 1) * QC)
                        load_toeplitz(it, g, h)
                sp.wait_ge(x1_stored, 16 * GI * (g + 1))

                def load_x1c(n, k):
                    sp.dma_start(x1c[:, k, :], x1_dram[bass.ds(n, 1), :, 2 * SP_ * k:2 * SP_ * (k + 1)].rearrange("a p q -> p (a q)")).then_inc(x1c_loaded[k], 16)

                def store_out(n, k):
                    sp.wait_ge(sum_ready, NK * n + k + 2)
                    sp.dma_start(out[bass.ds(n, 1), :, 2 * SP_ * k:2 * SP_ * (k + 1)].rearrange("a p q -> p (a q)"), x1c[:, k, :]).then_inc(out_stored[k], 16)

                for k in range(NK):
                    load_x1c(g * GI, k)
                with sp.Fori(0, GI - 1) as i:
                    for k in range(NK):
                        store_out(g * GI + i, k)
                        sp.wait_ge(out_stored[k], 16 * (g * GI + i) + 16)
                        load_x1c(g * GI + i + 1, k)
                for k in range(NK):
                    store_out(g * GI + GI - 1, k)
                wait_apart(sp, *((out_stored[k], 16 * GI * (g + 1)) for k in range(NK)))

        @block.tensor
        def _(pe):
            mm = nc.tensor.matmul
            pe.wait_ge(consts_loaded, 16 * N_CONST)
            for k in range(TAPS_H):
                last = mm(ps[:, 7, TAPS_W * k:TAPS_W * (k + 1)], w10s[:, k, :], w8s, start=True, stop=True)
            last.then_inc(prep_pe, 1)
            pe.wait_ge(prep, 8)
            nc.tensor.transpose(ps[0:TROWS, 6, 0:P], wc_rows, ident[:, :]).then_inc(prep_pe, 1)
            pe.wait_ge(prep, 10)

            def group_mean(n, c, at):
                pe.wait_ge(at["stats"], n + 1)
                mm(ps[:, 7, 0:1], gmat[:, :], gn[:, c, 0:1], start=True, stop=True).then_inc(at["mean"], 1)

            def group_var(n, c, at):
                pe.wait_ge(at["spread"], n + 1)
                mm(ps[:, 7, 0:1], gmat[:, :], gn[:, c, 4:5], start=True, stop=True).then_inc(at["var"], 1)

            def xT_chunks(n, ks, again):
                for k in ks:
                    if k in (0, NCH // 2):
                        pe.wait_ge(xn_ready, 2 * n + (1 if k == 0 else 2))
                    if k < 2 and again:
                        pe.wait_ge(t5T_ready, NCH * (n - 1) + k + 3)
                    if k >= 2:
                        pe.wait_ge(xT_ready, NCH * n + k - 1)
                    for j in range(3):
                        q = (3 * k + j) * P
                        last = nc.tensor.transpose(ps[:, k % 2, j * P:(j + 1) * P], xn[:, q:q + P], ident[:, :])
                    last.then_inc(xT_psum, 1)

            def t1T(n):
                pe.wait_ge(t1_ready, n + 1)
                mm(ps[0:NS * NR, 7, 0:P], t1s[:, :, :].rearrange("p s r -> p (s r)"), ident_b[:, :], start=True, stop=True).then_inc(t1T_psum, 1)

            def t5T_chunk(n, k, after_x1):
                if k % (NCH // NM) == 0:
                    pe.wait_ge(t5_ready, NM * n + k * NM // NCH + 1)
                if k < 4 and after_x1:
                    pe.wait_ge(x1_ready, NCH * (n - 1) + (5 + k if k < 2 else k + 1))
                if k in (2, 3) and not after_x1:
                    pe.wait_ge(xT_ready, NCH * n + k + 3)
                if k >= 4:
                    pe.wait_ge(t5T_ready, NCH * n + k - 3)
                for j in range(3):
                    q = (3 * k + j) * P
                    last = nc.tensor.transpose(ps[:, t5T_bank(k), j * P:(j + 1) * P], t5[:, q:q + P], ident[:, :])
                last.then_inc(t5T_psum, 1)

            def t11_chunk(n, k):
                if k == 0:
                    pe.wait_ge(taps_ready, n + 1)
                if k >= 2:
                    pe.wait_ge(t12_ready, NCH * n + k - 1)
                for j in range(3):
                    q = (3 * k + j) * P
                    last = mm(ps[:, 4 + k % 2, j * P:(j + 1) * P], taps[:, q:q + P], wcT[:, :], start=True, stop=True)
                last.then_inc(t11_psum, 1)

            def m_chunk(n, k):
                pe.wait_ge(t5T_ready, NCH * n + k + 1)
                pe.wait_ge(t12_ready, NCH * n + k + 1)
                for j in range(3):
                    q = (3 * k + j) * P
                    last = mm(ps[:, 6, 0:P], t5T[:, q:q + P], xT[:, q:q + P], start=(k == 0 and j == 0), stop=(k == NCH - 1 and j == 2))
                if k == NCH - 1:
                    last.then_inc(m_psum, 1)

            def x1_chunk(n, k, prev, nxt):
                if k == 0:
                    pe.wait_ge(g_ready, n + 1)
                if k < 2 and prev:
                    pe.wait_ge(tile_ready, NCH * (n - 1) + k + 3)
                if k in (2, 3) and nxt:
                    pe.wait_ge(xT_ready, NCH * (n + 1) + k + 3)
                if k >= 4:
                    pe.wait_ge(x1_ready, NCH * n + k - 3)
                mm(ps[:, x1_bank(k), 0:CH], gi_sb[:, :], xin[:, bass.ds(slot(n) + k * CH, CH)], start=True, stop=True).then_inc(x1_psum, 1)

            def tile_chunk(n, k, after):
                if k in (0, NCH // 2):
                    pe.wait_ge(xpad_ready, 2 * n + (1 if k == 0 else 2))
                if k < 2:
                    pe.wait_ge(t12_ready, NCH * (n + after) + k + 5)
                if k in (2, 3) and after:
                    pe.wait_ge(t5T_ready, NCH * (n + 1) + k + 3)
                if k in (2, 3) and not after:
                    pe.wait_ge(x1_ready, NCH * n + k + 3)
                if k >= 4:
                    pe.wait_ge(tile_ready, NCH * n + k - 3)
                for j in range(4):
                    t = 4 * k + j
                    r = TR * (TH - 1 - t % TH)
                    src = xpad[:, t // TH, r:r + TR, :].rearrange("p r w -> p (r w)")
                    last = nc.tensor.transpose(ps[0:TP, tile_bank(k), j * P:(j + 1) * P], src, ident[:, :])
                last.then_inc(tile_psum, 1)

            def layer0(n, prev, nxt, nxt2):
                for k in range(NCH):
                    t11_chunk(n, k)
                    if prev and k == 0:
                        pe.wait_ge(cst_ready, n)
                        pe.wait_ge(gnx["var_eps"], n + 1 + (1 if nxt else 0))
                        group_mean(n - 1, 1, gn1)
                    if prev and k == 1:
                        group_var(n - 1, 1, gn1)
                    if k:
                        m_chunk(n, k - 1)
                    if nxt and k >= 2:
                        xT_chunks(n + 1, (k - 2,), True)
                m_chunk(n, NCH - 1)
                if nxt:
                    xT_chunks(n + 1, (NCH - 2, NCH - 1), True)
                pe.wait_ge(m_ready, n + 1)
                mm(ps[:, 6, 0:P], w6s[:, :], m_sb[:, :], start=True, stop=True).then_inc(g_psum, 1)
                if prev:
                    for k in range(4):
                        tile_chunk(n - 1, k, 1)
                    pe.wait_ge(gn1["var_eps"], n)
                if nxt:
                    pe.wait_ge(gnx["var_eps"], n + 2)
                    t1T(n + 1)
                if prev:
                    for k in range(4, NCH):
                        tile_chunk(n - 1, k, 1)
                if nxt:
                    pe.wait_ge(t1row_ready, n + 2)
                pe.wait_ge(gs_ready, n + 1)
                mm(ps[:, 7, 0:1], g_sb[:, :], kept[:, 1:2], start=True, stop=True).then_inc(cst_psum, 1)
                for k in range(NCH):
                    x1_chunk(n, k, prev, nxt)
                if nxt2:
                    pe.wait_ge(cst_ready, n + 1)
                    group_mean(n + 2, 0, gnx)
                if nxt:
                    for k in range(NCH):
                        t5T_chunk(n + 1, k, True)
                        if nxt2 and k == 1:
                            group_var(n + 2, 0, gnx)
            with pe.Fori(0, NG) as g:
                n0 = g * GI
                group_mean(n0, 0, gnx)
                group_var(n0, 0, gnx)
                xT_chunks(n0, range(NCH), False)
                pe.wait_ge(gnx["var_eps"], n0 + 1)
                t1T(n0)
                pe.wait_ge(t1row_ready, n0 + 1)
                group_mean(n0 + 1, 0, gnx)
                group_var(n0 + 1, 0, gnx)
                for k in range(NCH):
                    t5T_chunk(n0, k, False)
                layer0(n0, False, True, True)
                with pe.Fori(1, GI - 2) as i:
                    layer0(n0 + i, True, True, True)
                layer0(n0 + GI - 2, True, True, False)
                layer0(n0 + GI - 1, True, False, False)
                group_mean(n0 + GI - 1, 1, gn1)
                group_var(n0 + GI - 1, 1, gn1)
                for k in range(NCH):
                    tile_chunk(n0 + GI - 1, k, 0)
                wait_apart(pe, (gn1["var_eps"], n0 + GI), (tile_ready, NCH * (n0 + GI)))

                with pe.Fori(0, C // UC) as it:
                    for u in range(UC):
                        if u % QC == 0:
                            pe.wait_ge(toep_loaded[u // QC], 16 * (g * (C // UC) + it) + 16)
                        pe.wait_ge((even_free, odd_free)[u % 2], (g * (C // UC) + it) * (UC // 2) + u // 2 + 1)
                        T = shared[0:TP, u * TB:(u + 1) * TB]
                        o = ps[0:TP, u, 0:TG].rearrange("p (s t) -> p s t", t=TH)
                        r = tiles[:, bass.ds(it * UC + u, 1), :].rearrange("p a (s t) -> p (a s) t", t=TH)
                        mm(o, T[:, TP:2 * TP], r, start=True, stop=False)
                        mm(o[:, :, 0:TH - 1], T[:, 0:TP], r[:, :, 1:TH], start=False, stop=False)
                        mm(o[:, :, 1:TH], T[:, 2 * TP:3 * TP], r[:, :, 0:TH - 1], start=False, stop=True).then_inc(conv_psum, 1)
                wait_apart(pe, (even_free, (g + 1) * (C // 2) + UC // 2), (odd_free, (g + 1) * (C // 2) + UC // 2))

                def z_tiles(s):
                    pe.wait_ge(normed_ready, s + 1)
                    for h in range(2):
                        for t in range(ST):
                            last = nc.tensor.transpose(ps[:, h, t * TP:(t + 1) * TP], normed[:, h * ST + t, :], ident[0:TP, 0:TP])
                    last.then_inc(z_psum, 1)

                def up(s, j):
                    if j == 0:
                        pe.wait_ge(z_ready, s + 1)
                    if j >= 2:
                        pe.wait_ge(h_ready, NJ * s + j - 1)
                    for h in range(2):
                        last = mm(ps[:, 2 + 2 * (j % 2) + h, 0:SP_], w1s[:, j * P:(j + 1) * P], zT[:, h, :], start=True, stop=True)
                    last.then_inc(h_psum, 1)

                def down(s, j):
                    pe.wait_ge(h_ready, NJ * s + j + 1)
                    for h in range(2):
                        last = mm(ps[:, 6 + h, 0:SP_], w2s[:, j, :], hid[:, j % 2, h * SP_:(h + 1) * SP_], start=(j == 0), stop=(j == NJ - 1))
                    if j == NJ - 1:
                        last.then_inc(y_psum, 1)

                def step(s, more):
                    up(s, 0)
                    up(s, 1)
                    pe.wait_ge(y_ready, s + 1)
                    down(s, 0)
                    up(s, 2)
                    down(s, 1)
                    up(s, 3)
                    if more:
                        z_tiles(s + 1)
                    down(s, 2)
                    down(s, 3)

                z_tiles(NK * n0)
                with pe.Fori(0, GI - 1) as i:
                    for k in range(NK):
                        step(NK * (n0 + i) + k, True)
                for k in range(NK):
                    step(NK * (n0 + GI - 1) + k, k < NK - 1)
                pe.wait_ge(y_ready, NK * (n0 + GI) + 1)

        @block.gpsimd
        def _(pool):
            pool.wait_ge(prep, 6)
            pool.dma_start(bass.AP(rvec, 0, [[RL, C], [1, RL]]), spread).then_inc(rvec_stored, 16)
            pool.dma_start(bass.AP(t1pad, 0, [[P, 1 + NS * NR], [1, P]]), zero_frame).then_inc(frame_stored, 16)
            nc.gpsimd.memset(minus_half[:, :], -0.5).then_inc(half_ready, 1)
            pool.wait_ge(half_ready, 1)
            pool.wait_ge(consts_loaded, 16 * N_CONST)

            def gn_power(n, c, at):
                pool.wait_ge(at["var_eps"], n + 1)
                nc.gpsimd.tensor_tensor(gn[:, c, 5:6], gn[:, c, 5:6], minus_half[:, 0:1], ALU.pow).then_inc(at["rstd"], 1)

            def weigh(n):
                for h in range(NM):
                    part = slice(HW // NM * h, HW // NM * (h + 1))
                    pool.wait_ge(min_done, NM * n + h + 1)
                    nc.gpsimd.tensor_tensor(t5[:, part], t5[:, part], p5[:, part], ALU.mult).then_inc(t5_ready, 1)

            def zero_edges(n):
                pool.wait_ge(taps_loaded, 16 * TAPS_H * (n + 1))
                rows = taps.rearrange("t (r w) -> t r w", w=W)
                for side in range(2):
                    cols = rows[:, :, side * (W - EDGE):side * (W - EDGE) + EDGE]
                    last = nc.gpsimd.tensor_tensor(cols, cols, edge[:, side * EDGE:(side + 1) * EDGE].unsqueeze(1).to_broadcast([TROWS, H, EDGE]), ALU.mult)
                last.then_inc(taps_ready, 1)

            def ln_power(s):
                pool.wait_ge(ln_var_eps, s + 1)
                nc.gpsimd.tensor_tensor(lnr[:, 0, :], lnr[:, 0, :], minus_half[0:TP, :], ALU.pow).then_inc(ln_rstd, 1)

            def residual(n, s, k):
                pool.wait_ge(x1c_loaded[k], 16 * n + 16)
                pool.wait_ge(y_ready, s + 2)
                xk = x1c[:, k, :].rearrange("p (r h w) -> p h r w", h=2, w=HALF)
                nc.gpsimd.tensor_tensor(xk, xk, mlp.rearrange("p (h r w) -> p h r w", h=2, w=HALF), ALU.add).then_inc(sum_ready, 1)

            with pool.Fori(0, NG) as g:
                n0 = g * GI
                gn_power(n0, 0, gnx)
                weigh(n0)
                gn_power(n0 + 1, 0, gnx)
                zero_edges(n0)

                def layer0(n, prev, nxt, nxt2):
                    if prev:
                        gn_power(n - 1, 1, gn1)
                    if nxt:
                        weigh(n + 1)
                    if nxt2:
                        gn_power(n + 2, 0, gnx)
                    if nxt:
                        zero_edges(n + 1)

                layer0(n0, False, True, True)
                with pool.Fori(1, GI - 2) as i:
                    layer0(n0 + i, True, True, True)
                layer0(n0 + GI - 2, True, True, False)
                gn_power(n0 + GI - 2, 1, gn1)
                gn_power(n0 + GI - 1, 1, gn1)
                ln_power(NK * n0)
                with pool.Fori(0, GI - 1) as i:
                    for k in range(NK):
                        ln_power(NK * (n0 + i) + k + 1)
                        residual(n0 + i, NK * (n0 + i) + k, k)
                for k in range(NK):
                    if k < NK - 1:
                        ln_power(NK * (n0 + GI - 1) + k + 1)
                    residual(n0 + GI - 1, NK * (n0 + GI - 1) + k, k)

        @block.scalar
        def _(act):
            def copy(out_, in_):
                return nc.scalar.activation(out_, in_, ACT.Identity)

            def normalise(n, again):
                wait_apart(act, (gnx["ready"], n + 1), *([(min_done, NM * n)] if again else []))
                for h in range(2):
                    q = h * (HW // 2)
                    nc.scalar.activation(xn[:, q:q + HW // 2], xin[:, bass.ds(slot(n) + q, HW // 2)], ACT.Identity,
                                         scale=gn[:, 0, 5:6], bias=gn[:, 0, 6:7]).then_inc(xn_ready, 1)

            def xT_copies(n, ks):
                for k in ks:
                    act.wait_ge(xT_psum, NCH * n + k + 1)
                    copy(xT[:, k * CH:(k + 1) * CH], ps[:, k % 2, 0:CH]).then_inc(xT_ready, 1)

            def backwards(h, c):
                full = xpad[:, h, :, :]
                last = (H - 1) * PW + PW - 1 - c
                return bass.AP(full.tensor, full.offset + last, [full.ap[0], [-PW, H], [-1, PW - HALO]])

            def pad(n, h):
                if h == 0:
                    wait_apart(act, (gn1["ready"], n + 1))
                v = xin[:, bass.ds(slot(n), HW)].rearrange("p (r w) -> p r w", w=W)
                to, cols = ((backwards(0, HALO), v[:, :, 0:PW - HALO]), (backwards(1, 0), v[:, :, HALF - HALO:W]))[h]
                nc.scalar.activation(to, cols, ACT.Identity, scale=gn[:, 1, 5:6], bias=gn[:, 1, 6:7]).then_inc(xpad_ready, 1)

            def tile_copies(n, i):
                for k in range(NCH):
                    wait_apart(act, (tile_psum, NCH * n + k + 1))
                    dst = tiles[:, :, bass.ds(i * TI + 4 * k, 4)].rearrange("p c t -> p t c")
                    copy(dst, ps[0:TP, tile_bank(k), 0:4 * P].rearrange("p (t c) -> p t c", c=C)).then_inc(tile_ready, 1)

            def t5T_copies(n):
                for k in range(NCH):
                    act.wait_ge(t5T_psum, NCH * n + k + 1)
                    copy(t5T[:, k * CH:(k + 1) * CH], ps[:, t5T_bank(k), 0:CH]).then_inc(t5T_ready, 1)

            def layer0(n, i, prev, nxt, nxt2):
                for k in range(NCH):
                    if prev and k < 2:
                        pad(n - 1, k)
                if nxt:
                    xT_copies(n + 1, range(NCH))
                if prev:
                    tile_copies(n - 1, i - 1)
                for k in range(NCH):
                    if k == 0:
                        wait_apart(act, (x1_psum, NCH * n + 1), (cst_ready, n + 1))
                    else:
                        wait_apart(act, (x1_psum, NCH * n + k + 1))
                    nc.scalar.activation(xin[:, bass.ds(slot(n) + k * CH, CH)], ps[:, x1_bank(k), 0:CH], ACT.Identity,
                                         bias=cst[:, :]).then_inc(x1_ready, 1)
                if nxt:
                    t5T_copies(n + 1)
                if nxt2:
                    normalise(n + 2, True)

            act.wait_ge(consts_loaded, 16 * N_CONST)
            with act.Fori(0, NG) as g:
                n0 = g * GI
                normalise(n0, False)
                xT_copies(n0, range(NCH))
                normalise(n0 + 1, True)
                t5T_copies(n0)
                layer0(n0, 0, False, True, True)
                with act.Fori(1, GI - 2) as i:
                    layer0(n0 + i, i, True, True, True)
                layer0(n0 + GI - 2, GI - 2, True, True, False)
                layer0(n0 + GI - 1, GI - 1, True, False, False)
                for h in range(2):
                    pad(n0 + GI - 1, h)
                tile_copies(n0 + GI - 1, GI - 1)

                with act.Fori(0, C // UC) as it:
                    for u in range(0, UC, 2):
                        wait_apart(act, (conv_psum, g * C + it * UC + u + 1))
                        nc.scalar.activation(tiles[:, bass.ds(it * UC + u, 1), :].rearrange("p a t -> p (a t)"), ps[0:TP, u, 0:TG],
                                             ACT.Identity, bias=dwb[:, bass.ds(it * UC + u, 1)]).then_inc(even_free, 1)

                def step(s):
                    for j in range(NJ):
                        act.wait_ge(h_psum, NJ * s + j + 1)
                        nc.scalar.activation(hid[:, j % 2, :].rearrange("p (h q) -> p h q", h=2), ps[:, 2 + 2 * (j % 2):4 + 2 * (j % 2), 0:SP_],
                                             ACT.Gelu_apprx_tanh, bias=b1_cols[:, j:j + 1]).then_inc(h_ready, 1)
                    act.wait_ge(y_psum, s + 1)
                    act.wait_ge(sum_ready, s + 1)
                    nc.scalar.activation(mlp.rearrange("p (h q) -> p h q", h=2), ps[:, 6:8, 0:SP_], ACT.Identity,
                                         scale=ls_col, bias=lsb2_col).then_inc(y_ready, 1)

                with act.Fori(0, GI) as i:
                    for k in range(NK):
                        step(NK * (n0 + i) + k)
                wait_apart(act, *((out_stored[k], 16 * (n0 + GI)) for k in range(NK)))

        @block.vector
        def _(dve):
            v = nc.vector
            v.memset(spread, 0.0).then_inc(prep, 1)
            v.memset(zero_frame, 0.0).then_inc(prep, 1)
            v.memset(xpad[:, :, :, :], 0.0).then_inc(prep, 1)
            v.memset(gn[:, :, :], 0.0).then_inc(prep, 1)
            v.memset(t1s[:, :, :], 0.0).then_inc(prep, 1)
            dve.sem_inc(even_free, UC // 2)
            dve.sem_inc(odd_free, UC // 2)
            for s in (y_ready, sum_ready, z_psum):
                dve.sem_inc(s, 1)
            dve.wait_ge(consts_loaded, 16 * N_CONST)
            dve.wait_ge(prep, 5)
            first = 2 * TP - KC * PW - KC
            v.tensor_copy(spread[:, first:first + K * PW].rearrange("p (y x) -> p y x", x=PW)[:, :, 0:K],
                          dws.rearrange("p (y x) -> p y x", x=K)).then_inc(prep, 1)
            dve.wait_ge(prep_pe, 1)
            v.tensor_copy(wc_sb, ps[:, 7, 0:NTAP]).then_inc(prep, 1)
            dve.wait_ge(prep, 7)
            v.tensor_copy(wc_part[:, 0, 0:NTAP], wc_sb).then_inc(wc_split, 1)
            dve.wait_ge(wc_split, 1)
            v.tensor_tensor(wc_rest, wc_sb, wc_part[:, 0, 0:NTAP], ALU.subtract).then_inc(wc_split, 1)
            dve.wait_ge(wc_split, 2)
            v.tensor_copy(wc_part[:, 1, 0:NTAP], wc_rest).then_inc(wc_split, 1)
            dve.wait_ge(wc_split, 3)
            v.tensor_tensor(wc_part[:, 2, 0:NTAP], wc_rest, wc_part[:, 1, 0:NTAP], ALU.subtract).then_inc(wc_split, 1)
            dve.wait_ge(wc_split, 4)
            rows = wc_rows.rearrange("o (k l j) -> o l k j", k=TAPS_H, l=NPL)
            for l, s in enumerate(s for s, parts in enumerate(SETS) for _ in range(parts)):
                last = v.tensor_copy(rows[:, l], wc_part[:, s, 0:NTAP].rearrange("o (k j) -> o k j", j=TAPS_W))
            last.then_inc(prep, 1)
            v.tensor_copy(ident_b[:, :], ident[:, :]).then_inc(prep, 1)
            dve.wait_ge(prep_pe, 2)
            v.tensor_copy(wcT[:, 1:P], ps[0:TROWS, 6, 0:P - 1])
            v.tensor_copy(wcT[:, 0:1], ps[0:TROWS, 6, P - 1:P]).then_inc(prep, 1)
            v.tensor_tensor(lsb2_col, ls_col, b2_col, ALU.mult).then_inc(prep, 1)
            dve.wait_ge(frame_stored, 16)
            dve.wait_ge(rvec_stored, 16)

            def moments(n, k, s, at):
                v.bn_stats(s[:, k, :], xin[:, bass.ds(slot(n) + k * CH, CH)]).then_inc(at["part"], 1)

            def aggregate(n, c, s, at):
                wait_apart(dve, (at["part"], NCH * (n + 1)))
                v.bn_aggr(gn[:, c, 0:2], s[:, :, :]).then_inc(at["stats"], 1)

            def gn_deviation(n, c, at):
                a = gn[:, c, :]
                dve.wait_ge(at["mean"], n + 1)
                v.tensor_scalar(a[:, 2:3], ps[:, 7, 0:1], -1.0, None, ALU.mult).then_inc(at["neg"], 1)
                dve.wait_ge(at["neg"], n + 1)
                v.tensor_tensor(a[:, 3:4], a[:, 0:1], a[:, 2:3], ALU.add).then_inc(at["dev"], 1)
                dve.wait_ge(at["dev"], n + 1)
                v.tensor_tensor(a[:, 3:4], a[:, 3:4], a[:, 3:4], ALU.mult).then_inc(at["square"], 1)
                dve.wait_ge(at["square"], n + 1)
                v.tensor_tensor(a[:, 4:5], a[:, 3:4], a[:, 1:2], ALU.add).then_inc(at["spread"], 1)

            def gn_variance(n, c, at):
                dve.wait_ge(at["var"], n + 1)
                v.tensor_scalar(gn[:, c, 5:6], ps[:, 7, 0:1], GN_EPS, None, ALU.add).then_inc(at["var_eps"], 1)

            def gn_bias(n, c, at):
                dve.wait_ge(at["rstd"], n + 1)
                v.tensor_tensor(gn[:, c, 6:7], gn[:, c, 2:3], gn[:, c, 5:6], ALU.mult).then_inc(at["ready"], 1)

            def stats_x(n):
                wait_apart(dve, (x_loaded, 16 * n + 16))
                for k in range(NCH):
                    moments(n, k, st1, gnx)
                aggregate(n, 0, st1, gnx)

            def gn_x(n):
                gn_deviation(n, 0, gnx)
                gn_variance(n, 0, gnx)
                gn_bias(n, 0, gnx)

            def keep(n):
                v.tensor_copy(kept[:, :], gn[:, 0, 5:7]).then_inc(kept_ready, 1)

            def shifted_min(n, h, again):
                dve.wait_ge(xn_ready, 2 * n + (1 if 2 * (h + 1) <= NM else 2))
                if again and h == 0:
                    dve.wait_ge(t5T_psum, NCH * n)
                a, o = (u[:, HW // NM * h:HW // NM * (h + 1)].rearrange("p (r w) -> p r w", w=W) for u in (xn, t5))
                v.tensor_tensor(o[:, :, 1:W], a[:, :, 1:W], a[:, :, 0:W - 1], ALU.min)
                v.tensor_tensor(o[:, :, 0:1], a[:, :, 0:1], a[:, :, W - 1:W], ALU.min).then_inc(min_done, 1)

            def channel_max(n, k):
                dve.wait_ge(xT_ready, NCH * n + k + 1)
                v.tensor_reduce(t1[:, 3 * k:3 * k + 3], xT[:, CH * k:CH * (k + 1)].rearrange("p (a c) -> p a c", c=P), AX_X, ALU.max).then_inc(t1_whole, 1)

            def split_t1(n):
                dve.wait_ge(t1_whole, NCH * (n + 1))
                v.tensor_copy(t1s[:, 0, 0:NT], t1[:, :]).then_inc(t1_high, 1)
                dve.wait_ge(t1_high, n + 1)
                v.tensor_tensor(t1s[:, 1, 0:NT], t1[:, :], t1s[:, 0, 0:NT], ALU.subtract)
                v.tensor_tensor(t1rest[:, :], t1[:, :], t1s[:, 0, 0:NT], ALU.subtract).then_inc(t1_left, 1)
                dve.wait_ge(t1_left, n + 1)
                v.tensor_tensor(t1s[:, 2, 0:NT], t1rest[:, :], t1s[:, 1, 0:NT], ALU.subtract).then_inc(t1_ready, 1)

            def t1_rows(n):
                dve.wait_ge(t1T_psum, n + 1)
                v.tensor_copy(t1row[:, :], ps[0:NS * NR, 7, 0:P]).then_inc(t1row_ready, 1)

            def layer0(n, prev, nxt, nxt2):
                if prev:
                    gn_deviation(n - 1, 1, gn1)
                for k in range(NCH):
                    dve.wait_ge(t11_psum, NCH * n + k + 1)
                    q = k * CH
                    v.tensor_tensor(xT[:, q:q + CH], xT[:, q:q + CH], ps[:, 4 + k % 2, 0:CH], ALU.max).then_inc(t12_ready, 1)
                    if prev and k == 0:
                        gn_variance(n - 1, 1, gn1)
                    if prev and k == 1:
                        gn_bias(n - 1, 1, gn1)
                    if nxt and 1 <= k < NM:
                        shifted_min(n + 1, k - 1, True)
                    if nxt and k >= 3:
                        channel_max(n + 1, k - 3)
                dve.wait_ge(m_psum, n + 1)
                v.tensor_copy(m_sb[:, :], ps[:, 6, 0:P]).then_inc(m_ready, 1)
                if nxt:
                    channel_max(n + 1, 3)
                dve.wait_ge(g_psum, n + 1)
                v.tensor_scalar(g_sb[:, :], ps[:, 6, 0:P], SCALE, None, ALU.mult).then_inc(gs_ready, 1)
                if nxt:
                    channel_max(n + 1, 4)
                    channel_max(n + 1, 5)
                    split_t1(n + 1)
                dve.wait_ge(gs_ready, n + 1)
                dve.wait_ge(kept_ready, n + 1)
                v.scalar_tensor_tensor(out=gi_sb[:, :], in0=g_sb[:, :], scalar=kept[:, 0:1], in1=ident[:, :],
                                       op0=ALU.mult, op1=ALU.add).then_inc(g_ready, 1)
                if nxt:
                    t1_rows(n + 1)
                    shifted_min(n + 1, NM - 1, True)
                dve.wait_ge(cst_psum, n + 1)
                v.tensor_copy(cst[:, :], ps[:, 7, 0:1]).then_inc(cst_ready, 1)
                if nxt:
                    keep(n + 1)

                def moments_x1(ks):
                    for k in ks:
                        wait_apart(dve, (x1_ready, NCH * n + k + 1))
                        moments(n, k, st2, gn1)

                if nxt2:
                    stats_x(n + 2)
                    moments_x1((0, 1))
                    gn_deviation(n + 2, 0, gnx)
                    moments_x1((2, 3))
                    gn_variance(n + 2, 0, gnx)
                    moments_x1((4,))
                    gn_bias(n + 2, 0, gnx)
                    moments_x1((5,))
                else:
                    moments_x1(range(NCH))
                aggregate(n, 1, st2, gn1)

            with dve.Fori(0, NG) as g:
                n0 = g * GI
                stats_x(n0)
                gn_x(n0)
                dve.wait_ge(gnx["ready"], n0 + 1)
                keep(n0)
                for h in range(NM):
                    shifted_min(n0, h, False)
                for k in range(NCH):
                    channel_max(n0, k)
                split_t1(n0)
                t1_rows(n0)
                stats_x(n0 + 1)
                gn_x(n0 + 1)
                layer0(n0, False, True, True)
                with dve.Fori(1, GI - 2) as i:
                    layer0(n0 + i, True, True, True)
                layer0(n0 + GI - 2, True, True, False)
                layer0(n0 + GI - 1, True, False, False)
                gn_deviation(n0 + GI - 1, 1, gn1)
                gn_variance(n0 + GI - 1, 1, gn1)
                gn_bias(n0 + GI - 1, 1, gn1)

                with dve.Fori(0, C // UC) as it:
                    for u in range(1, UC, 2):
                        dve.wait_ge(conv_psum, g * C + it * UC + u + 1)
                        v.tensor_scalar(tiles[:, bass.ds(it * UC + u, 1), :].rearrange("p a t -> p (a t)"), ps[0:TP, u, 0:TG],
                                        dwb[:, bass.ds(it * UC + u, 1)], None, ALU.add).then_inc(odd_free, 1)
                wait_apart(dve, (even_free, (g + 1) * (C // 2) + UC // 2), (odd_free, (g + 1) * (C // 2) + UC // 2))

                def step(i, s, k):
                    idx = [(h * ST + t, i * TI + h * TH + ST * k + t) for h in range(2) for t in range(ST)]

                    def tile(m):
                        return tiles[:, :, bass.ds(m, 1)].rearrange("p c a -> p (c a)")

                    for j, m in idx:
                        last = v.bn_stats(lnst[:, j, :], tile(m))
                    last.then_inc(ln_part, 1)
                    wait_apart(dve, (ln_part, s + 1))
                    for j, m in idx:
                        last = v.bn_aggr(lnmv[:, j, :], lnst[:, j, :])
                    last.then_inc(ln_aggr, 1)
                    dve.wait_ge(ln_aggr, s + 1)
                    v.tensor_scalar(lnr[:, 0, :], lnmv[:, :, 1], LN_EPS, None, ALU.add).then_inc(ln_var_eps, 1)
                    dve.wait_ge(ln_rstd, s + 1)
                    v.scalar_tensor_tensor(out=lnr[:, 1, :], in0=lnmv[:, :, 0], scalar=-1.0, in1=lnr[:, 0, :],
                                           op0=ALU.mult, op1=ALU.mult).then_inc(ln_ready, 1)
                    dve.wait_ge(ln_ready, s + 1)
                    dve.wait_ge(z_psum, s + 1)
                    for j, m in idx:
                        last = v.tensor_scalar(normed[:, j, :], tile(m), lnr[:, 0, j:j + 1], lnr[:, 1, j:j + 1], ALU.mult, ALU.add)
                    last.then_inc(normed_ready, 1)
                    dve.wait_ge(z_psum, s + 2)
                    for h in range(2):
                        last = v.tensor_scalar(zT[:, h, :].rearrange("p (r w) -> p r w", w=HALF),
                                               ps[:, h, 0:ST * TP].rearrange("p (r w) -> p r w", w=PW)[:, :, HALO:HALO + HALF],
                                               g_col, b_col, ALU.mult, ALU.add)
                    last.then_inc(z_ready, 1)

                with dve.Fori(0, GI) as i:
                    for k in range(NK):
                        step(i, NK * (n0 + i) + k, k)


_INS = ["x", "p5_w", "w6t", "w8", "w10t", "dw_rev", "dw_b", "ln_g", "ln_b", "w1t", "b1", "w2t", "b2", "ls", "ident", "gmat", "edge"]


def kernel(**inputs):
    import numpy as np
    import concourse.bacc as bacc
    from concourse.bass_utils import run_bass_kernel_spmd

    a = {k: np.asarray(v) for k, v in inputs.items()}
    N, C, H, W = a["x"].shape
    col = lambda v: v.reshape(-1, 1)
    arrays = {
        "x": a["x"].reshape(N, C, H * W),
        "p5_w": a["L0_conv_p5_w"].reshape(C, H * W),
        "w6t": a["L0_conv_w6"].T,
        "w8": a["L0_conv_w8"].reshape(C // 2, -1),
        "w10t": a["L0_conv_w10"].T.reshape(C // 2, 3, C),
        "dw_rev": a["L1_conv_dw_w"].reshape(C, -1)[:, ::-1],
        "dw_b": a["L1_conv_dw_b"],
        "ln_g": col(a["L1_conv_ln_g"]),
        "ln_b": col(a["L1_conv_ln_b"]),
        "w1t": a["L1_conv_w1"].T,
        "b1": a["L1_conv_b1"].reshape(-1, C).T,
        "w2t": a["L1_conv_w2"].T,
        "b2": col(a["L1_conv_b2"]),
        "ls": col(a["L1_conv_ls"]),
        "ident": np.eye(C, dtype=np.float32),
        "gmat": np.kron(np.eye(32, dtype=np.float32), np.full((C // 32, C // 32), 32 / C, np.float32)),
    }
    cols = np.r_[0:6, W - 6:W]
    inside = np.stack([(cols + 3 * j - 6 >= 0) & (cols + 3 * j - 6 < W) for j in range(5)])
    arrays["edge"] = np.tile(inside, (24, 1)).astype(np.float32)
    nc = bacc.Bacc("TRN2", target_bir_lowering=False, num_devices=1)
    named, args = {}, []
    for name in _INS:
        v = np.ascontiguousarray(arrays[name])
        named[f"in_{name}"] = v
        args.append(nc.dram_tensor(f"in_{name}", v.shape, mybir.dt.from_np(v.dtype), kind="ExternalInput").ap())
    out = nc.dram_tensor("out_0", (N, C, H * W), F32, kind="ExternalOutput").ap()
    build(nc, *args, out)
    r = run_bass_kernel_spmd(nc, [named], core_ids=[0])
    return r.results[0]["out_0"].reshape(N, C, H, W)
```

```python
from contextlib import ExitStack

import concourse.bass as bass
from concourse import mybir

F32 = mybir.dt.float32
BF16 = mybir.dt.bfloat16
ALU = mybir.AluOpType
ACT = mybir.ActivationFunctionType
AX_X = mybir.AxisListType.X


def build(nc, x, p5_w, w6t, w8, w10t, dw_rev, dw_b, ln_g, ln_b, w1t, b1, w2t, b2, ls, ident_in, gmat_in, edge_in, out):
    N, C, HW = x.shape
    W = H = 48
    P = 128
    GI = 8
    NG = N // GI
    XS = 3
    CH = 384
    NCH = HW // CH
    NT = HW // P
    NM = 3
    HID = w1t.shape[1]
    NJ = HID // P
    HALF, HALO = W // 2, 3
    PW = HALF + 2 * HALO
    TR = 4
    TP = TR * PW
    TH = H // TR
    TI = 2 * TH
    TG = GI * TI
    K = 7
    KC = K // 2
    TAPS_H, TAPS_W = 3, 5
    NTAP = TAPS_H * TAPS_W
    EDGE = 3 * (TAPS_W // 2)
    NS = 3
    SETS = (NS, NS, 2)
    NPL = sum(SETS)
    TROWS = NTAP * NPL
    NR = NT + 1
    RL = 4 * TP
    TB = 3 * TP
    QC = 4
    NQ = 4
    UC = NQ * QC
    BANKS = 8
    NK = 3
    SR = H // NK
    ST = SR // TR
    SP_ = SR * HALF
    GN_EPS, LN_EPS = 1e-5, 1e-5
    SCALE = -1.0 / (float(C) ** 0.5 * float(HW) ** 0.5)
    assert PW * KC + KC <= TP and SP_ == CH and 2 * SP_ * NK == HW

    t1pad = nc.dram_tensor("t1pad", (1 + len(SETS) * NS * NR, P), BF16, kind="Internal")
    rvec = nc.dram_tensor("rvec", (C, RL), F32, kind="Internal")
    x1_dram = nc.dram_tensor("x1_dram", (N, C, HW), F32, kind="Internal").ap()

    with ExitStack() as ctx:
        def sb(name, shape, dtype=F32):
            return ctx.enter_context(nc.sbuf_tensor(name, shape, dtype))

        def sem(name):
            return ctx.enter_context(nc.semaphore(name))

        tiles = sb("tiles", [TP, C, TG])
        xin = sb("xin", [P, XS * HW])
        xn = sb("xn", [P, HW])
        t5 = sb("t5", [P, HW])
        p5 = sb("p5", [P, HW])
        xT = sb("xT", [P, HW])
        t5T = sb("t5T", [P, HW])
        xpad = sb("xpad", [P, 2, H, PW])
        shared = sb("shared", [P, 2 * QC * TB])
        ident = sb("ident", [P, P])
        gmat = sb("gmat", [P, P])
        w6s = sb("w6s", [P, P])
        wcT = sb("wcT", [TROWS, P], BF16)
        w1s = sb("w1s", [P, HID])
        w2s = sb("w2s", [P, NJ, P])
        dwb = sb("dwb", [TP, C])
        vecs = sb("vecs", [P, 12])
        m_sb = sb("m_sb", [P, P])
        gi_sb = sb("gi_sb", [P, P])
        t1 = sb("t1", [P, NT])
        t1s = sb("t1s", [P, NS, NR], BF16)
        t1rest = sb("t1rest", [P, NT])
        t1row = sb("t1row", [NS * NR, P], BF16)
        ident_b = sb("ident_b", [P, P], BF16)
        edge = sb("edge", [TROWS, 2 * EDGE])
        st1 = sb("st1", [P, NCH, 6])
        st2 = sb("st2", [P, NCH, 6])
        gn = sb("gn", [P, 2, 7])
        kept = sb("kept", [P, 2])
        cst = sb("cst", [P, 1])
        lnst = sb("lnst", [TP, 2 * ST, 6])
        lnmv = sb("lnmv", [TP, 2 * ST, 2])
        lnr = sb("lnr", [TP, 2, 2 * ST])
        minus_half = sb("minus_half", [P, 2 * ST])
        ps = ctx.enter_context(nc.psum_tensor("ps", [P, 8, 512], F32))

        taps = shared[0:TROWS, 0:HW // 2].bitcast(BF16)
        normed = shared[0:TP, 0:2 * ST * C].rearrange("p (t c) -> p t c", c=C)
        zT = shared[:, 2 * ST * C:2 * ST * C + 2 * SP_].rearrange("p (h q) -> p h q", h=2)
        toeplitz = [buf[0:TP, first:first + QC * TB] for buf, first in ((shared, 0), (shared, QC * TB), (xT, 0), (t5T, 0))]
        hid = xT[:, 0:4 * SP_].rearrange("p (b q) -> p b q", b=2)
        mlp = xT[:, 4 * SP_:6 * SP_]
        x1c = t5T[:, :].rearrange("p (k q) -> p k q", k=NK)
        g_col, b_col, b2_col, ls_col, lsb2_col = (vecs[:, i:i + 1] for i in range(5))
        b1_cols = vecs[:, 5:5 + NJ]
        dws = t5[:, 0:K * K]
        spread = t5[:, 64:64 + RL]
        w8s = t5[0:C // 2, 1000:1000 + TAPS_W]
        w10s = xT[0:C // 2, 0:TAPS_H * P].rearrange("c (k o) -> c k o", k=TAPS_H)
        wc_sb = t5[:, 1100:1100 + NTAP]
        wc_part = t5[:, 1200:1200 + 24].bitcast(BF16).rearrange("o (s t) -> o s t", s=NS)
        wc_rest = t5[:, 1232:1232 + NTAP]
        wc_rows = t5[:, 1300:1300 + TROWS]
        zero_frame = t5[0:1 + NS * NR, 1500:1500 + P // 2].bitcast(BF16)

        consts_loaded = sem("consts_loaded")
        group_consts_loaded = sem("group_consts_loaded")
        prep = sem("prep")
        prep_pe = sem("prep_pe")
        wc_split = sem("wc_split")
        half_ready = sem("half_ready")
        frame_stored, rvec_stored = sem("frame_stored"), sem("rvec_stored")
        x_loaded = [sem(f"x_loaded{h}") for h in range(2)]
        GN_STEPS = ("part", "stats", "mean", "neg", "dev", "square", "spread", "var", "var_eps", "rstd", "ready")
        gnx = {step: sem(f"gnx_{step}") for step in GN_STEPS}
        gn1 = {step: sem(f"gn1_{step}") for step in GN_STEPS}
        xn_ready = sem("xn_ready")
        min_done, t5_ready = sem("min_done"), sem("t5_ready")
        xT_psum, xT_ready = sem("xT_psum"), sem("xT_ready")
        t1_ready, t1T_psum, t1row_ready = sem("t1_ready"), sem("t1T_psum"), sem("t1row_ready")
        t1_whole, t1_high, t1_left = sem("t1_whole"), sem("t1_high"), sem("t1_left")
        t1_stored, taps_loaded = sem("t1_stored"), sem("taps_loaded")
        taps_ready = sem("taps_ready")
        t5T_psum, t5T_ready = sem("t5T_psum"), sem("t5T_ready")
        t11_psum, t12_ready = sem("t11_psum"), sem("t12_ready")
        m_psum, m_ready = sem("m_psum"), sem("m_ready")
        g_psum, g_ready = sem("g_psum"), sem("g_ready")
        kept_ready = sem("kept_ready")
        cst_psum, cst_ready = sem("cst_psum"), sem("cst_ready")
        x1_psum, x1_ready = sem("x1_psum"), sem("x1_ready")
        x1_stored = sem("x1_stored")
        xpad_ready = sem("xpad_ready")
        tile_psum, tile_ready = sem("tile_psum"), sem("tile_ready")
        toep_loaded = [sem(f"toep_loaded{h}") for h in range(NQ)]
        conv_psum = sem("conv_psum")
        even_free, odd_free = sem("even_free"), sem("odd_free")
        LN_STEPS = ("part", "aggr", "var_eps", "rstd", "ready", "normed", "z_psum", "z_ready")
        ln = {step: sem(f"ln_{step}") for step in LN_STEPS}
        ln_first = {step: sem(f"ln_first_{step}") for step in LN_STEPS}
        h_psum, h_ready = sem("h_psum"), sem("h_ready")
        y_psum, y_ready = sem("y_psum"), sem("y_ready")
        x1c_loaded = [sem(f"x1c_loaded{k}") for k in range(NK)]
        sum_ready = sem("sum_ready")
        out_stored = [sem(f"out_stored{k}") for k in range(NK)]

        E = mybir.EngineType
        passed = {e: sem(f"passed_{n}") for e, n in ((E.SP, "sync"), (E.PE, "tensor"), (E.Activation, "scalar"), (E.DVE, "vector"))}

        N_CONST = 14
        block = ctx.enter_context(nc.Block())

        def wait_apart(eng, *waits):
            for s, count in waits:
                eng.wait_ge(s, count)
            eng.sem_inc(passed[eng.engine], 1)

        def xT_bank(k):
            return k % 4

        def tile_bank(k):
            return (4, 5, 2, 3)[k % 4]

        def last_tile_bank(k):
            return (4, 5, 2, 3, 0, 1)[k]

        def x1_bank(k):
            return (2, 3, 0, 1)[k % 4]

        t5T_bank = x1_bank

        def slot(n):
            return (n % XS) * HW

        def backwards(h, c):
            full = xpad[:, h, :, :]
            last = (H - 1) * PW + PW - 1 - c
            return bass.AP(full.tensor, full.offset + last, [full.ap[0], [-PW, H], [-1, PW - HALO]])

        def pad_operands(n, h):
            v = xin[:, bass.ds(slot(n), HW)].rearrange("p (r w) -> p r w", w=W)
            return ((backwards(0, HALO), v[:, :, 0:PW - HALO]), (backwards(1, 0), v[:, :, HALF - HALO:W]))[h]

        def tiles_of(i, k):
            return tiles[:, :, bass.ds(i * TI + 4 * k, 4)].rearrange("p c t -> p t c")

        def tile_source(bank):
            return ps[0:TP, bank, 0:4 * P].rearrange("p (t c) -> p t c", c=C)

        @block.sync
        def _(sp):
            def const(dst, src):
                sp.dma_start(dst, src).then_inc(consts_loaded, 16)

            def load_half(h, at, image):
                part = slice(h * HW // 2, (h + 1) * HW // 2)
                sp.dma_start(xin[:, bass.ds(at + h * HW // 2, HW // 2)], image[:, part]).then_inc(x_loaded[h], 16)

            for h in range(2):
                load_half(h, 0, x[0])
            for dst, src in ((gmat[:, :], gmat_in), (ident[:, :], ident_in)):
                sp.dma_start(dst, src).then_inc(group_consts_loaded, 16)
            const(dws, dw_rev)
            const(w8s, w8)
            const(w10s, w10t)
            const(edge[:, :], edge_in)
            const(w6s[:, :], w6t)
            const(p5[:, :], p5_w)
            const(w1s[:, :], w1t)
            const(w2s[:, :, :], w2t.rearrange("(j p) c -> p j c", p=P))
            const(dwb[:, :], bass.AP(dw_b.tensor, 0, [[0, TP], [1, C]]))
            const(g_col, ln_g)
            const(b_col, ln_b)
            const(b2_col, b2)
            const(ls_col, ls)
            const(b1_cols, b1)
            for n in range(1, XS):
                for h in range(2):
                    sp.wait_ge(x_loaded[h], 16 * n)
                    load_half(h, n * HW, x[n])
                if n == 1:
                    sp.wait_ge(prep, 6)
                    sp.dma_start(bass.AP(rvec, 0, [[RL, C], [1, RL]]), spread).then_inc(rvec_stored, 16)
                    sp.dma_start(bass.AP(t1pad, 0, [[P, 1 + NS * NR], [1, P]]), zero_frame).then_inc(frame_stored, 16)

            def load_x(n):
                for h in range(2):
                    sp.wait_ge(x_loaded[h], 16 * n)
                    load_half(h, slot(n), x[bass.ds(n % N, 1)].rearrange("a p q -> p (a q)"))

            def t1_round_trip(n):
                sp.wait_ge(t1row_ready, n + 1)
                sp.dma_start(bass.AP(t1pad, P, [[P, NS * NR], [NS * NR * P, len(SETS)], [1, P]]),
                             t1row[:, :].unsqueeze(1).to_broadcast([NS * NR, len(SETS), P])).then_inc(t1_stored, 16)
                sp.wait_ge(t1_stored, 16 * (n + 1))
                rows = NPL * TAPS_W
                for k in range(TAPS_H):
                    sp.dma_start(taps[k * rows:(k + 1) * rows],
                                 bass.AP(t1pad, P + (2 * k - 2) * W - EDGE, [[NR * P, NPL], [3, TAPS_W], [1, HW]])).then_inc(taps_loaded, 16)

            def store_x1(n):
                sp.wait_ge(x1_ready, NCH * n + NCH)
                sp.dma_start(x1_dram[bass.ds(n, 1)].rearrange("a p q -> p (a q)"), xin[:, bass.ds(slot(n), HW)]).then_inc(x1_stored, 16)

            def load_toeplitz(it, g, h):
                src = bass.AP(rvec, (it * UC + h * QC) * RL + 1, [[1, TP], [RL, QC], [1, TB]])
                sp.dma_start(toeplitz[h].rearrange("p (c j) -> p c j", c=QC), src).then_inc(toep_loaded[h], 16)

            with sp.Fori(0, NG) as g:
                def free_slot(n):
                    sp.wait_ge(x1_stored, 16 * n + 16)
                    sp.wait_ge(xpad_ready, 2 * n + 2)

                t1_round_trip(g * GI)
                t1_round_trip(g * GI + 1)
                store_x1(g * GI)
                with sp.Fori(1, GI - 2) as i:
                    free_slot(g * GI + i - 1)
                    load_x(g * GI + i + 2)
                    t1_round_trip(g * GI + i + 1)
                    store_x1(g * GI + i)
                for i in (GI - 2, GI - 1):
                    n = g * GI + i
                    with sp.If(g < NG - 1):
                        free_slot(n - 1)
                        load_x(n + 2)
                    if i < GI - 1:
                        t1_round_trip(n + 1)
                    else:
                        sp.wait_ge(t11_psum, NCH * GI * (g + 1))
                        sp.wait_ge(rvec_stored, 16)
                        for h in range(NQ):
                            if h == 2:
                                sp.wait_ge(m_psum, GI * (g + 1))
                            load_toeplitz(0, g, h)
                    store_x1(n)
                with sp.If(g < NG - 1):
                    free_slot(g * GI + GI - 1)
                    load_x(g * GI + GI + 2)
                with sp.Fori(1, C // UC) as it:
                    for h in range(NQ):
                        sp.wait_ge(conv_psum, g * C + (it - 1) * UC + (h + 1) * QC)
                        load_toeplitz(it, g, h)
                sp.wait_ge(x1_stored, 16 * GI * (g + 1))
                sp.wait_ge(conv_psum, (g + 1) * C)

                def load_x1c(n, k):
                    sp.dma_start(x1c[:, k, :], x1_dram[bass.ds(n, 1), :, 2 * SP_ * k:2 * SP_ * (k + 1)].rearrange("a p q -> p (a q)")).then_inc(x1c_loaded[k], 16)

                def store_out(n, k):
                    sp.wait_ge(sum_ready, NK * n + k + 2)
                    sp.dma_start(out[bass.ds(n, 1), :, 2 * SP_ * k:2 * SP_ * (k + 1)].rearrange("a p q -> p (a q)"), x1c[:, k, :]).then_inc(out_stored[k], 16)

                for k in range(NK):
                    load_x1c(g * GI, k)
                with sp.Fori(0, GI - 1) as i:
                    for k in range(NK):
                        store_out(g * GI + i, k)
                        sp.wait_ge(out_stored[k], 16 * (g * GI + i) + 16)
                        load_x1c(g * GI + i + 1, k)
                for k in range(NK):
                    store_out(g * GI + GI - 1, k)
                wait_apart(sp, *((out_stored[k], 16 * GI * (g + 1)) for k in range(NK)))

        @block.tensor
        def _(pe):
            mm = nc.tensor.matmul
            def group_mean(n, c, at, bank=7):
                pe.wait_ge(at["stats"], n + 1)
                mm(ps[:, bank, 0:1], gmat[:, :], gn[:, c, 0:1], start=True, stop=True).then_inc(at["mean"], 1)

            def group_var(n, c, at, bank=7):
                pe.wait_ge(at["spread"], n + 1)
                mm(ps[:, bank, 0:1], gmat[:, :], gn[:, c, 4:5], start=True, stop=True).then_inc(at["var"], 1)

            pe.wait_ge(group_consts_loaded, 32)
            group_mean(0, 0, gnx)
            group_var(0, 0, gnx)
            pe.wait_ge(gnx["var_eps"], 1)
            pe.wait_ge(consts_loaded, 16 * N_CONST)
            for k in range(TAPS_H):
                last = mm(ps[:, 7, TAPS_W * k:TAPS_W * (k + 1)], w10s[:, k, :], w8s, start=True, stop=True)
            last.then_inc(prep_pe, 1)
            pe.wait_ge(prep, 8)
            nc.tensor.transpose(ps[0:TROWS, 6, 0:P], wc_rows, ident[:, :]).then_inc(prep_pe, 1)
            pe.wait_ge(prep, 12)

            def xT_chunks(n, ks, again):
                for k in ks:
                    if k in (0, NCH // 2):
                        pe.wait_ge(xn_ready, 2 * n + (1 if k == 0 else 2))
                    if k < 4 and again:
                        pe.wait_ge(t5T_ready, NCH * (n - 1) + k + 3)
                    if k >= 4:
                        pe.wait_ge(xT_ready, NCH * n + k - 3)
                    for j in range(3):
                        q = (3 * k + j) * P
                        last = nc.tensor.transpose(ps[:, xT_bank(k), j * P:(j + 1) * P], xn[:, q:q + P], ident[:, :])
                    last.then_inc(xT_psum, 1)

            def t1T(n):
                pe.wait_ge(t1_ready, n + 1)
                mm(ps[0:NS * NR, 7, 0:P], t1s[:, :, :].rearrange("p s r -> p (s r)"), ident_b[:, :], start=True, stop=True).then_inc(t1T_psum, 1)

            def t5T_chunk(n, k, after_x1):
                if k % (NCH // NM) == 0:
                    pe.wait_ge(t5_ready, NM * n + k * NM // NCH + 1)
                if k < 4 and after_x1:
                    pe.wait_ge(x1_ready, NCH * (n - 1) + (5 + k if k < 2 else k + 1))
                if k < 4 and not after_x1:
                    pe.wait_ge(xT_ready, NCH * n + k + 3)
                if k >= 4:
                    pe.wait_ge(t5T_ready, NCH * n + k - 3)
                for j in range(3):
                    q = (3 * k + j) * P
                    last = nc.tensor.transpose(ps[:, t5T_bank(k), j * P:(j + 1) * P], t5[:, q:q + P], ident[:, :])
                last.then_inc(t5T_psum, 1)

            def t11_chunk(n, k):
                if k % (NCH // NM) == 0:
                    pe.wait_ge(taps_ready, NM * n + k * NM // NCH + 1)
                if k >= 2:
                    pe.wait_ge(t12_ready, NCH * n + k - 1)
                for j in range(3):
                    q = (3 * k + j) * P
                    last = mm(ps[:, 4 + k % 2, j * P:(j + 1) * P], taps[:, q:q + P], wcT[:, :], start=True, stop=True)
                last.then_inc(t11_psum, 1)

            def m_chunk(n, k):
                pe.wait_ge(t5T_ready, NCH * n + k + 1)
                pe.wait_ge(t12_ready, NCH * n + k + 1)
                for j in range(3):
                    q = (3 * k + j) * P
                    last = mm(ps[:, 6, 0:P], t5T[:, q:q + P], xT[:, q:q + P], start=(k == 0 and j == 0), stop=(k == NCH - 1 and j == 2))
                if k == NCH - 1:
                    last.then_inc(m_psum, 1)

            def x1_chunk(n, k, prev, nxt):
                if k < 2 and prev:
                    pe.wait_ge(tile_ready, NCH * (n - 1) + k + 3)
                if k in (2, 3) and nxt:
                    pe.wait_ge(xT_ready, NCH * (n + 1) + k + 3)
                if k >= 4:
                    pe.wait_ge(x1_ready, NCH * n + k - 3)
                mm(ps[:, x1_bank(k), 0:CH], gi_sb[:, :], xin[:, bass.ds(slot(n) + k * CH, CH)], start=True, stop=True).then_inc(x1_psum, 1)

            def tile_chunk(n, k, after, nxt=False):
                if not after:
                    pe.wait_ge(xpad_ready, 2 * n + 2)
                elif k in (0, NCH // 2):
                    pe.wait_ge(xpad_ready, 2 * n + (1 if k == 0 else 2))
                if k < 2:
                    pe.wait_ge(t12_ready, NCH * (n + after) + k + 5)
                if k in (2, 3) and after and nxt:
                    pe.wait_ge(xT_ready, NCH * (n + 2) + k + 1)
                if k in (2, 3) and after and not nxt:
                    pe.wait_ge(t5T_ready, NCH * (n + 1) + k + 3)
                if k >= 2 and not after:
                    pe.wait_ge(x1_ready, NCH * n + NCH)
                if k >= 4 and after:
                    pe.wait_ge(tile_ready, NCH * n + k - 3)
                for j in range(4):
                    t = 4 * k + j
                    r = TR * (TH - 1 - t % TH)
                    src = xpad[:, t // TH, r:r + TR, :].rearrange("p r w -> p (r w)")
                    last = nc.tensor.transpose(ps[0:TP, tile_bank(k) if after else last_tile_bank(k), j * P:(j + 1) * P], src, ident[:, :])
                last.then_inc(tile_psum, 1)

            def layer0(n, prev, nxt, nxt2):
                for k in range(NCH):
                    if k:
                        t11_chunk(n, k)
                    if prev and k == 2:
                        pe.wait_ge(cst_ready, n)
                        pe.wait_ge(gnx["var_eps"], n + 1 + (1 if nxt else 0))
                        group_mean(n - 1, 1, gn1)
                    if k:
                        m_chunk(n, k - 1)
                    if prev and k == 2:
                        group_var(n - 1, 1, gn1)
                    if nxt and k >= 2:
                        xT_chunks(n + 1, (k - 2,), True)
                m_chunk(n, NCH - 1)
                if nxt:
                    xT_chunks(n + 1, (NCH - 2, NCH - 1), True)
                pe.wait_ge(m_ready, n + 1)
                mm(ps[:, 6, 0:P], w6s[:, :], m_sb[:, :], start=True, stop=True).then_inc(g_psum, 1)
                if prev:
                    for k in range(4):
                        tile_chunk(n - 1, k, 1, nxt)
                    pe.wait_ge(gn1["var_eps"], n)
                if nxt:
                    pe.wait_ge(gnx["var_eps"], n + 2)
                    t1T(n + 1)
                if prev:
                    for k in range(4, NCH):
                        tile_chunk(n - 1, k, 1, nxt)
                if nxt:
                    pe.wait_ge(t1row_ready, n + 2)
                pe.wait_ge(g_ready, n + 1)
                mm(ps[:, 7, 0:1], gi_sb[:, :], kept[:, 0:1], start=True, stop=True).then_inc(cst_psum, 1)
                for k in range(NCH):
                    x1_chunk(n, k, prev, nxt)
                if nxt2:
                    pe.wait_ge(cst_ready, n + 1)
                    group_mean(n + 2, 0, gnx)
                if nxt:
                    for k in range(NCH):
                        t5T_chunk(n + 1, k, True)
                        if k == 3:
                            t11_chunk(n + 1, 0)
                        if nxt2 and k == 1:
                            group_var(n + 2, 0, gnx)
            with pe.Fori(0, NG) as g:
                n0 = g * GI
                xT_chunks(n0, range(NCH), False)
                for k in range(NCH):
                    t5T_chunk(n0, k, False)
                t1T(n0)
                pe.wait_ge(t1row_ready, n0 + 1)
                group_mean(n0 + 1, 0, gnx)
                group_var(n0 + 1, 0, gnx)
                t11_chunk(n0, 0)
                layer0(n0, False, True, True)
                with pe.Fori(1, GI - 2) as i:
                    layer0(n0 + i, True, True, True)
                layer0(n0 + GI - 2, True, True, False)
                layer0(n0 + GI - 1, True, False, False)
                group_mean(n0 + GI - 1, 1, gn1)
                group_var(n0 + GI - 1, 1, gn1)
                for k in range(NCH):
                    tile_chunk(n0 + GI - 1, k, 0)
                wait_apart(pe, (gn1["var_eps"], n0 + GI), (tile_ready, NCH * (n0 + GI)))

                with pe.Fori(0, C // UC) as it:
                    for u in range(UC):
                        if u % QC == 0:
                            pe.wait_ge(toep_loaded[u // QC], 16 * (g * (C // UC) + it) + 16)
                        pe.wait_ge((even_free, odd_free)[u % 2], (g * (C // UC) + it) * (UC // 2) + u // 2 + 1)
                        T = toeplitz[u // QC][:, u % QC * TB:(u % QC + 1) * TB]
                        o = ps[0:TP, u % BANKS, 0:TG].rearrange("p (s t) -> p s t", t=TH)
                        r = tiles[:, bass.ds(it * UC + u, 1), :].rearrange("p a (s t) -> p (a s) t", t=TH)
                        mm(o, T[:, TP:2 * TP], r, start=True, stop=False)
                        mm(o[:, :, 0:TH - 1], T[:, 0:TP], r[:, :, 1:TH], start=False, stop=False)
                        mm(o[:, :, 1:TH], T[:, 2 * TP:3 * TP], r[:, :, 0:TH - 1], start=False, stop=True).then_inc(conv_psum, 1)
                wait_apart(pe, (even_free, (g + 1) * (C // 2) + BANKS // 2), (odd_free, (g + 1) * (C // 2) + BANKS // 2))

                def z_half(h, at, count):
                    pe.wait_ge(at["normed"], count)
                    for t in range(ST):
                        last = nc.tensor.transpose(ps[:, h, t * TP:(t + 1) * TP], normed[:, h * ST + t, :], ident[0:TP, 0:TP])
                    return last

                def z_tiles(s):
                    z_half(0, ln, s + 1)
                    z_half(1, ln, s + 1).then_inc(ln["z_psum"], 1)

                def up(s, j, first=False):
                    if j >= 2:
                        pe.wait_ge(h_ready, NJ * s + j - 1)
                    for h in range(2):
                        if j == 0 and h == 0 and first:
                            pe.wait_ge(ln_first["z_ready"], g + 1)
                        elif j == 0 and h == (1 if first else 0):
                            pe.wait_ge(ln["z_ready"], s + 1)
                        last = mm(ps[:, 2 + 2 * (j % 2) + h, 0:SP_], w1s[:, j * P:(j + 1) * P], zT[:, h, :], start=True, stop=True)
                    last.then_inc(h_psum, 1)

                def down(s, j):
                    pe.wait_ge(h_ready, NJ * s + j + 1)
                    for h in range(2):
                        last = mm(ps[:, 6 + h, 0:SP_], w2s[:, j, :], hid[:, j % 2, h * SP_:(h + 1) * SP_], start=(j == 0), stop=(j == NJ - 1))
                    if j == NJ - 1:
                        last.then_inc(y_psum, 1)

                def step(s, more, ahead=None, first=False):
                    up(s, 0, first)
                    if ahead is not None:
                        group_mean(ahead, 0, gnx, bank=0)
                    up(s, 1)
                    if ahead is not None:
                        group_var(ahead, 0, gnx, bank=0)
                    pe.wait_ge(y_ready, s + 1)
                    down(s, 0)
                    up(s, 2)
                    down(s, 1)
                    up(s, 3)
                    if ahead is not None:
                        pe.wait_ge(gnx["var_eps"], ahead + 1)
                    if more:
                        z_tiles(s + 1)
                    down(s, 2)
                    down(s, 3)

                z_half(0, ln_first, g + 1).then_inc(ln_first["z_psum"], 1)
                z_half(1, ln, NK * n0 + 1).then_inc(ln["z_psum"], 1)
                for k in range(NK):
                    step(NK * n0 + k, True, first=(k == 0))
                with pe.Fori(1, GI - 1) as i:
                    for k in range(NK):
                        step(NK * (n0 + i) + k, True)
                s = NK * (n0 + GI - 1)
                step(s, True)
                with pe.If(g < NG - 1):
                    step(s + 1, True, n0 + GI)
                with pe.Else():
                    step(s + 1, True)
                step(s + 2, False)
                pe.wait_ge(y_ready, NK * (n0 + GI) + 1)

        @block.gpsimd
        def _(pool):
            nc.gpsimd.memset(minus_half[:, :], -0.5).then_inc(half_ready, 1)
            pool.wait_ge(half_ready, 1)

            def gn_power(n, c, at):
                pool.wait_ge(at["var_eps"], n + 1)
                nc.gpsimd.tensor_tensor(gn[:, c, 5:6], gn[:, c, 5:6], minus_half[:, 0:1], ALU.pow).then_inc(at["rstd"], 1)

            def weigh(n):
                for h in range(NM):
                    part = slice(HW // NM * h, HW // NM * (h + 1))
                    pool.wait_ge(min_done, NM * n + h + 1)
                    nc.gpsimd.tensor_tensor(t5[:, part], t5[:, part], p5[:, part], ALU.mult).then_inc(t5_ready, 1)

            def zero_edges(n, hs=range(NM)):
                pool.wait_ge(taps_loaded, 16 * TAPS_H * (n + 1))
                sides = taps.rearrange("t (r b e) -> t r b e", r=H, e=EDGE)[:, :, 0:W // EDGE:W // EDGE - 1, :]
                inside = edge[:, :].rearrange("t (b e) -> t b e", b=2).unsqueeze(1).to_broadcast([TROWS, H // NM, 2, EDGE])
                for h in hs:
                    part = sides[:, H // NM * h:H // NM * (h + 1)]
                    nc.gpsimd.tensor_tensor(part, part, inside, ALU.mult).then_inc(taps_ready, 1)

            def ln_power(at, count, cols):
                pool.wait_ge(at["var_eps"], count)
                nc.gpsimd.tensor_tensor(lnr[:, 0, cols], lnr[:, 0, cols], minus_half[0:TP, cols], ALU.pow).then_inc(at["rstd"], 1)

            def residual(n, s, k):
                pool.wait_ge(x1c_loaded[k], 16 * n + 16)
                pool.wait_ge(y_ready, s + 2)
                xk = x1c[:, k, :].rearrange("p (r h w) -> p h r w", h=2, w=HALF)
                nc.gpsimd.tensor_tensor(xk, xk, mlp.rearrange("p (h r w) -> p h r w", h=2, w=HALF), ALU.add).then_inc(sum_ready, 1)

            gn_power(0, 0, gnx)
            pool.wait_ge(consts_loaded, 16 * N_CONST)
            weigh(0)
            with pool.Fori(0, NG) as g:
                n0 = g * GI
                gn_power(n0 + 1, 0, gnx)
                zero_edges(n0)

                def layer0(n, prev, nxt, nxt2):
                    if prev:
                        gn_power(n - 1, 1, gn1)
                    if nxt:
                        weigh(n + 1)
                    if nxt:
                        zero_edges(n + 1, (0,))
                    if nxt2:
                        gn_power(n + 2, 0, gnx)
                    if nxt:
                        zero_edges(n + 1, range(1, NM))

                layer0(n0, False, True, True)
                with pool.Fori(1, GI - 2) as i:
                    layer0(n0 + i, True, True, True)
                layer0(n0 + GI - 2, True, True, False)
                gn_power(n0 + GI - 2, 1, gn1)
                gn_power(n0 + GI - 1, 1, gn1)
                ln_power(ln_first, g + 1, slice(0, ST))
                ln_power(ln, NK * n0 + 1, slice(ST, 2 * ST))
                with pool.Fori(0, GI - 1) as i:
                    for k in range(NK):
                        ln_power(ln, NK * (n0 + i) + k + 2, slice(0, 2 * ST))
                        residual(n0 + i, NK * (n0 + i) + k, k)
                for k in range(NK):
                    if k == 1:
                        with pool.If(g < NG - 1):
                            gn_power(n0 + GI, 0, gnx)
                    if k < NK - 1:
                        ln_power(ln, NK * (n0 + GI - 1) + k + 2, slice(0, 2 * ST))
                    residual(n0 + GI - 1, NK * (n0 + GI - 1) + k, k)
                    if k == 1:
                        with pool.If(g < NG - 1):
                            weigh(n0 + GI)

        @block.scalar
        def _(act):
            def copy(out_, in_):
                return nc.scalar.activation(out_, in_, ACT.Identity)

            def normalise(n, again):
                wait_apart(act, (gnx["ready"], n + 1), *([(min_done, NM * n)] if again else []))
                for h in range(2):
                    q = h * (HW // 2)
                    nc.scalar.activation(xn[:, q:q + HW // 2], xin[:, bass.ds(slot(n) + q, HW // 2)], ACT.Identity,
                                         scale=gn[:, 0, 5:6], bias=gn[:, 0, 6:7]).then_inc(xn_ready, 1)

            def xT_copies(n, ks):
                for k in ks:
                    act.wait_ge(xT_psum, NCH * n + k + 1)
                    copy(xT[:, k * CH:(k + 1) * CH], ps[:, xT_bank(k), 0:CH]).then_inc(xT_ready, 1)

            def pad(n, h):
                if h == 0:
                    wait_apart(act, (gn1["ready"], n + 1))
                to, cols = pad_operands(n, h)
                nc.scalar.activation(to, cols, ACT.Identity, scale=gn[:, 1, 5:6], bias=gn[:, 1, 6:7]).then_inc(xpad_ready, 1)

            def tile_copies(n, i):
                for k in range(NCH):
                    wait_apart(act, (tile_psum, NCH * n + k + 1))
                    copy(tiles_of(i, k), tile_source(tile_bank(k))).then_inc(tile_ready, 1)

            def t5T_copies(n, ks=range(NCH)):
                for k in ks:
                    act.wait_ge(t5T_psum, NCH * n + k + 1)
                    copy(t5T[:, k * CH:(k + 1) * CH], ps[:, t5T_bank(k), 0:CH]).then_inc(t5T_ready, 1)

            def layer0(n, i, prev, nxt, nxt2):
                for k in range(NCH):
                    if nxt:
                        xT_copies(n + 1, (k,))
                    if prev and k < 2:
                        pad(n - 1, k)
                if prev:
                    tile_copies(n - 1, i - 1)
                for k in range(NCH):
                    if k == 0:
                        wait_apart(act, (x1_psum, NCH * n + 1), (cst_ready, n + 1))
                    else:
                        wait_apart(act, (x1_psum, NCH * n + k + 1))
                    nc.scalar.activation(xin[:, bass.ds(slot(n) + k * CH, CH)], ps[:, x1_bank(k), 0:CH], ACT.Identity,
                                         bias=cst[:, :]).then_inc(x1_ready, 1)
                if nxt:
                    t5T_copies(n + 1)
                if nxt2:
                    normalise(n + 2, True)

            normalise(0, False)
            act.wait_ge(consts_loaded, 16 * N_CONST)
            xT_copies(0, range(NCH))
            t5T_copies(0)
            with act.Fori(0, NG) as g:
                n0 = g * GI
                normalise(n0 + 1, True)
                layer0(n0, 0, False, True, True)
                with act.Fori(1, GI - 2) as i:
                    layer0(n0 + i, i, True, True, True)
                layer0(n0 + GI - 2, GI - 2, True, True, False)
                layer0(n0 + GI - 1, GI - 1, True, False, False)
                pad(n0 + GI - 1, 0)
                for k in range(0, NCH, 2):
                    wait_apart(act, (tile_psum, NCH * (n0 + GI - 1) + k + 1))
                    copy(tiles_of(GI - 1, k), tile_source(last_tile_bank(k))).then_inc(tile_ready, 1)

                with act.Fori(0, C // UC) as it:
                    for u in range(0, UC, 2):
                        wait_apart(act, (conv_psum, g * C + it * UC + u + 1))
                        nc.scalar.activation(tiles[:, bass.ds(it * UC + u, 1), :].rearrange("p a t -> p (a t)"), ps[0:TP, u % BANKS, 0:TG],
                                             ACT.Identity, bias=dwb[:, bass.ds(it * UC + u, 1)]).then_inc(even_free, 1)

                def gelus(s, js):
                    for j in js:
                        act.wait_ge(h_psum, NJ * s + j + 1)
                        nc.scalar.activation(hid[:, j % 2, :].rearrange("p (h q) -> p h q", h=2), ps[:, 2 + 2 * (j % 2):4 + 2 * (j % 2), 0:SP_],
                                             ACT.Gelu_apprx_tanh, bias=b1_cols[:, j:j + 1]).then_inc(h_ready, 1)

                def scaled(s):
                    act.wait_ge(y_psum, s + 1)
                    act.wait_ge(sum_ready, s + 1)
                    nc.scalar.activation(mlp.rearrange("p (h q) -> p h q", h=2), ps[:, 6:8, 0:SP_], ACT.Identity,
                                         scale=ls_col, bias=lsb2_col).then_inc(y_ready, 1)

                def image(s, more):
                    for k in range(NK):
                        gelus(s + k, range(2, NJ) if k == 0 else range(NJ))
                        scaled(s + k)
                        if k == 1 and not more:
                            with act.If(g < NG - 1):
                                normalise(n0 + GI, True)
                    if more:
                        gelus(s + NK, range(2))

                gelus(NK * n0, range(2))
                with act.Fori(0, GI - 1) as i:
                    image(NK * (n0 + i), True)
                image(NK * (n0 + GI - 1), False)
                with act.If(g < NG - 1):
                    xT_copies(n0 + GI, range(4))
                    wait_apart(act, (sum_ready, NK * (n0 + GI) + 1))
                    xT_copies(n0 + GI, (4, 5))
                    for k in range(NK):
                        wait_apart(act, (out_stored[k], 16 * (n0 + GI)))
                        t5T_copies(n0 + GI, (2 * k, 2 * k + 1))

        @block.vector
        def _(dve):
            v = nc.vector
            v.memset(spread, 0.0).then_inc(prep, 1)
            v.memset(zero_frame, 0.0).then_inc(prep, 1)
            v.memset(xpad[:, :, :, :], 0.0).then_inc(prep, 1)
            v.memset(gn[:, :, :], 0.0).then_inc(prep, 1)
            v.memset(t1s[:, :, :], 0.0).then_inc(prep, 1)
            dve.sem_inc(even_free, BANKS // 2)
            dve.sem_inc(odd_free, BANKS // 2)
            for s in (y_ready, sum_ready, ln["z_psum"]):
                dve.sem_inc(s, 1)
            dve.wait_ge(prep, 5)

            def moments(n, k, s, at):
                v.bn_stats(s[:, k, :], xin[:, bass.ds(slot(n) + k * CH, CH)]).then_inc(at["part"], 1)

            def aggregate(n, c, s, at):
                wait_apart(dve, (at["part"], NCH * (n + 1)))
                v.bn_aggr(gn[:, c, 0:2], s[:, :, :]).then_inc(at["stats"], 1)

            def gn_deviation(n, c, at, bank=7):
                a = gn[:, c, :]
                dve.wait_ge(at["mean"], n + 1)
                v.tensor_scalar(a[:, 2:3], ps[:, bank, 0:1], -1.0, None, ALU.mult).then_inc(at["neg"], 1)
                dve.wait_ge(at["neg"], n + 1)
                v.tensor_tensor(a[:, 3:4], a[:, 0:1], a[:, 2:3], ALU.add).then_inc(at["dev"], 1)
                dve.wait_ge(at["dev"], n + 1)
                v.tensor_tensor(a[:, 3:4], a[:, 3:4], a[:, 3:4], ALU.mult).then_inc(at["square"], 1)
                dve.wait_ge(at["square"], n + 1)
                v.tensor_tensor(a[:, 4:5], a[:, 3:4], a[:, 1:2], ALU.add).then_inc(at["spread"], 1)

            def gn_variance(n, c, at, bank=7):
                dve.wait_ge(at["var"], n + 1)
                v.tensor_scalar(gn[:, c, 5:6], ps[:, bank, 0:1], GN_EPS, None, ALU.add).then_inc(at["var_eps"], 1)

            def gn_bias(n, c, at):
                dve.wait_ge(at["rstd"], n + 1)
                v.tensor_tensor(gn[:, c, 6:7], gn[:, c, 2:3], gn[:, c, 5:6], ALU.mult).then_inc(at["ready"], 1)

            def moments_x(n):
                for k in range(NCH):
                    if k % (NCH // 2) == 0:
                        wait_apart(dve, (x_loaded[k // (NCH // 2)], 16 * n + 16))
                    moments(n, k, st1, gnx)

            def stats_x(n):
                moments_x(n)
                aggregate(n, 0, st1, gnx)

            def gn_x(n, bank=7):
                gn_deviation(n, 0, gnx, bank)
                gn_variance(n, 0, gnx, bank)
                gn_bias(n, 0, gnx)

            def keep(n, again):
                if again:
                    dve.wait_ge(cst_ready, n)
                dve.wait_ge(gnx["ready"], n + 1)
                v.tensor_copy(kept[:, :], gn[:, 0, 2:6:3]).then_inc(kept_ready, 1)

            stats_x(0)
            gn_x(0)
            keep(0, False)

            dve.wait_ge(consts_loaded, 16 * N_CONST)
            first = 2 * TP - KC * PW - KC
            v.tensor_copy(spread[:, first:first + K * PW].rearrange("p (y x) -> p y x", x=PW)[:, :, 0:K],
                          dws.rearrange("p (y x) -> p y x", x=K)).then_inc(prep, 1)
            dve.wait_ge(prep_pe, 1)
            v.tensor_copy(wc_sb, ps[:, 7, 0:NTAP]).then_inc(prep, 1)
            dve.wait_ge(prep, 7)
            v.tensor_copy(wc_part[:, 0, 0:NTAP], wc_sb).then_inc(wc_split, 1)
            dve.wait_ge(wc_split, 1)
            v.tensor_tensor(wc_rest, wc_sb, wc_part[:, 0, 0:NTAP], ALU.subtract).then_inc(wc_split, 1)
            dve.wait_ge(wc_split, 2)
            v.tensor_copy(wc_part[:, 1, 0:NTAP], wc_rest).then_inc(wc_split, 1)
            dve.wait_ge(wc_split, 3)
            v.tensor_tensor(wc_part[:, 2, 0:NTAP], wc_rest, wc_part[:, 1, 0:NTAP], ALU.subtract).then_inc(wc_split, 1)
            dve.wait_ge(wc_split, 4)
            rows = wc_rows.rearrange("o (k l j) -> o l k j", k=TAPS_H, l=NPL)
            for l, s in enumerate(s for s, parts in enumerate(SETS) for _ in range(parts)):
                last = v.tensor_copy(rows[:, l], wc_part[:, s, 0:NTAP].rearrange("o (k j) -> o k j", j=TAPS_W))
            last.then_inc(prep, 1)
            v.tensor_copy(ident_b[:, :], ident[:, :]).then_inc(prep, 1)
            dve.wait_ge(prep_pe, 2)
            v.tensor_copy(wcT[:, 1:P], ps[0:TROWS, 6, 0:P - 1])
            v.tensor_copy(wcT[:, 0:1], ps[0:TROWS, 6, P - 1:P]).then_inc(prep, 1)
            v.tensor_tensor(lsb2_col, ls_col, b2_col, ALU.mult).then_inc(prep, 1)
            v.tensor_scalar(w6s[:, :], w6s[:, :], SCALE, None, ALU.mult).then_inc(prep, 1)
            dve.wait_ge(frame_stored, 16)
            dve.wait_ge(rvec_stored, 16)

            def shifted_min(n, h, again):
                dve.wait_ge(xn_ready, 2 * n + (1 if 2 * (h + 1) <= NM else 2))
                if again and h == 0:
                    dve.wait_ge(t5T_psum, NCH * n)
                a, o = (u[:, HW // NM * h:HW // NM * (h + 1)].rearrange("p (r w) -> p r w", w=W) for u in (xn, t5))
                v.tensor_tensor(o[:, :, 1:W], a[:, :, 1:W], a[:, :, 0:W - 1], ALU.min)
                v.tensor_tensor(o[:, :, 0:1], a[:, :, 0:1], a[:, :, W - 1:W], ALU.min).then_inc(min_done, 1)

            def channel_max(n, k):
                dve.wait_ge(xT_ready, NCH * n + k + 1)
                v.tensor_reduce(t1[:, 3 * k:3 * k + 3], xT[:, CH * k:CH * (k + 1)].rearrange("p (a c) -> p a c", c=P), AX_X, ALU.max).then_inc(t1_whole, 1)

            def split_t1(n):
                dve.wait_ge(t1_whole, NCH * (n + 1))
                v.tensor_copy(t1s[:, 0, 0:NT], t1[:, :]).then_inc(t1_high, 1)
                dve.wait_ge(t1_high, n + 1)
                v.tensor_tensor(t1s[:, 1, 0:NT], t1[:, :], t1s[:, 0, 0:NT], ALU.subtract)
                v.tensor_tensor(t1rest[:, :], t1[:, :], t1s[:, 0, 0:NT], ALU.subtract).then_inc(t1_left, 1)
                dve.wait_ge(t1_left, n + 1)
                v.tensor_tensor(t1s[:, 2, 0:NT], t1rest[:, :], t1s[:, 1, 0:NT], ALU.subtract).then_inc(t1_ready, 1)

            def t1_rows(n):
                dve.wait_ge(t1T_psum, n + 1)
                v.tensor_copy(t1row[:, :], ps[0:NS * NR, 7, 0:P]).then_inc(t1row_ready, 1)

            def moments_x1(n, ks):
                for k in ks:
                    wait_apart(dve, (x1_ready, NCH * n + k + 1))
                    moments(n, k, st2, gn1)

            def layer0(n, prev, nxt, nxt2):
                for k in range(NCH):
                    dve.wait_ge(t11_psum, NCH * n + k + 1)
                    q = k * CH
                    v.tensor_tensor(xT[:, q:q + CH], xT[:, q:q + CH], ps[:, 4 + k % 2, 0:CH], ALU.max).then_inc(t12_ready, 1)
                    if prev and k == 0:
                        moments_x1(n - 1, (NCH - 1,))
                        aggregate(n - 1, 1, st2, gn1)
                    if prev and k == 1:
                        gn_deviation(n - 1, 1, gn1)
                    if prev and k == 2:
                        gn_variance(n - 1, 1, gn1)
                    if nxt and k == 2:
                        shifted_min(n + 1, 0, True)
                    if prev and k == 2:
                        gn_bias(n - 1, 1, gn1)
                    if nxt and k == 3:
                        shifted_min(n + 1, 1, True)
                    if nxt and k >= 3:
                        channel_max(n + 1, k - 3)
                dve.wait_ge(m_psum, n + 1)
                v.tensor_copy(m_sb[:, :], ps[:, 6, 0:P]).then_inc(m_ready, 1)
                if nxt:
                    channel_max(n + 1, 3)
                if nxt:
                    channel_max(n + 1, 4)
                    channel_max(n + 1, 5)
                    split_t1(n + 1)
                dve.wait_ge(g_psum, n + 1)
                dve.wait_ge(kept_ready, n + 1)
                v.scalar_tensor_tensor(out=gi_sb[:, :], in0=ps[:, 6, 0:P], scalar=kept[:, 1:2], in1=ident[:, :],
                                       op0=ALU.mult, op1=ALU.add).then_inc(g_ready, 1)
                if nxt:
                    t1_rows(n + 1)
                    shifted_min(n + 1, NM - 1, True)
                dve.wait_ge(cst_psum, n + 1)
                v.tensor_tensor(cst[:, :], ps[:, 7, 0:1], kept[:, 0:1], ALU.subtract).then_inc(cst_ready, 1)
                if nxt and not nxt2:
                    keep(n + 1, True)
                if nxt2:
                    moments_x(n + 2)
                    keep(n + 1, True)
                    aggregate(n + 2, 0, st1, gnx)
                    moments_x1(n, (0, 1))
                    gn_deviation(n + 2, 0, gnx)
                    moments_x1(n, (2,))
                    gn_variance(n + 2, 0, gnx)
                    moments_x1(n, (3, 4))
                    gn_bias(n + 2, 0, gnx)
                else:
                    moments_x1(n, range(NCH - 1))

            for h in range(NM):
                shifted_min(0, h, False)

            with dve.Fori(0, NG) as g:
                n0 = g * GI
                for k in range(NCH):
                    channel_max(n0, k)
                split_t1(n0)
                t1_rows(n0)
                stats_x(n0 + 1)
                gn_x(n0 + 1)
                layer0(n0, False, True, True)
                with dve.Fori(1, GI - 2) as i:
                    layer0(n0 + i, True, True, True)
                layer0(n0 + GI - 2, True, True, False)
                layer0(n0 + GI - 1, True, False, False)
                moments_x1(n0 + GI - 1, (NCH - 1,))
                aggregate(n0 + GI - 1, 1, st2, gn1)
                gn_deviation(n0 + GI - 1, 1, gn1)
                gn_variance(n0 + GI - 1, 1, gn1)
                gn_bias(n0 + GI - 1, 1, gn1)
                to, cols = pad_operands(n0 + GI - 1, 1)
                wait_apart(dve, (gn1["ready"], n0 + GI))
                v.tensor_scalar(to, cols, gn[:, 1, 5:6], gn[:, 1, 6:7], ALU.mult, ALU.add).then_inc(xpad_ready, 1)
                for k in range(1, NCH, 2):
                    wait_apart(dve, (tile_psum, NCH * (n0 + GI - 1) + k + 1))
                    v.tensor_copy(tiles_of(GI - 1, k), tile_source(last_tile_bank(k))).then_inc(tile_ready, 1)

                with dve.Fori(0, C // UC) as it:
                    for u in range(1, UC, 2):
                        dve.wait_ge(conv_psum, g * C + it * UC + u + 1)
                        v.tensor_scalar(tiles[:, bass.ds(it * UC + u, 1), :].rearrange("p a t -> p (a t)"), ps[0:TP, u % BANKS, 0:TG],
                                        dwb[:, bass.ds(it * UC + u, 1)], None, ALU.add).then_inc(odd_free, 1)
                wait_apart(dve, (even_free, (g + 1) * (C // 2) + BANKS // 2), (odd_free, (g + 1) * (C // 2) + BANKS // 2))

                def tiles_of_step(i, k, h):
                    return [(h * ST + t, tiles[:, :, bass.ds(i * TI + h * TH + ST * k + t, 1)].rearrange("p c a -> p (c a)")) for t in range(ST)]

                def ln_variance(group, at, count):
                    cols = slice(group[0][0], group[-1][0] + 1)
                    for j, tile in group:
                        last = v.bn_stats(lnst[:, j, :], tile)
                    last.then_inc(at["part"], 1)
                    wait_apart(dve, (at["part"], count))
                    for j, _ in group:
                        last = v.bn_aggr(lnmv[:, j, :], lnst[:, j, :])
                    last.then_inc(at["aggr"], 1)
                    dve.wait_ge(at["aggr"], count)
                    v.tensor_scalar(lnr[:, 0, cols], lnmv[:, cols, 1], LN_EPS, None, ALU.add).then_inc(at["var_eps"], 1)

                def ln_apply(group, at, count):
                    cols = slice(group[0][0], group[-1][0] + 1)
                    dve.wait_ge(at["rstd"], count)
                    v.scalar_tensor_tensor(out=lnr[:, 1, cols], in0=lnmv[:, cols, 0], scalar=-1.0, in1=lnr[:, 0, cols],
                                           op0=ALU.mult, op1=ALU.mult).then_inc(at["ready"], 1)
                    dve.wait_ge(at["ready"], count)
                    for j, tile in group:
                        last = v.tensor_scalar(normed[:, j, :], tile, lnr[:, 0, j:j + 1], lnr[:, 1, j:j + 1], ALU.mult, ALU.add)
                    last.then_inc(at["normed"], 1)

                def z_half(h):
                    return v.tensor_scalar(zT[:, h, :].rearrange("p (r w) -> p r w", w=HALF),
                                           ps[:, h, 0:ST * TP].rearrange("p (r w) -> p r w", w=PW)[:, :, HALO:HALO + HALF],
                                           g_col, b_col, ALU.mult, ALU.add)

                def step(i, s, k):
                    group = tiles_of_step(i, k, 0) + tiles_of_step(i, k, 1)
                    ln_variance(group, ln, s + 1)
                    dve.wait_ge(ln["z_psum"], s + 1)
                    ln_apply(group, ln, s + 1)
                    dve.wait_ge(ln["z_psum"], s + 2)
                    z_half(0)
                    z_half(1).then_inc(ln["z_ready"], 1)

                halves = [(tiles_of_step(0, 0, 0), ln_first, g + 1), (tiles_of_step(0, 0, 1), ln, NK * n0 + 1)]
                for half in halves:
                    ln_variance(*half)
                for half in halves:
                    ln_apply(*half)
                dve.wait_ge(ln_first["z_psum"], g + 1)
                z_half(0).then_inc(ln_first["z_ready"], 1)
                dve.wait_ge(ln["z_psum"], NK * n0 + 2)
                z_half(1).then_inc(ln["z_ready"], 1)
                for k in range(1, NK):
                    step(0, NK * n0 + k, k)
                with dve.Fori(1, GI - 1) as i:
                    for k in range(NK):
                        step(i, NK * (n0 + i) + k, k)
                for k in range(NK):
                    step(GI - 1, NK * (n0 + GI - 1) + k, k)
                    with dve.If(g < NG - 1):
                        if k == 0:
                            stats_x(n0 + GI)
                        if k == 1:
                            gn_x(n0 + GI, bank=0)
                            keep(n0 + GI, True)
                        if k == 2:
                            for h in range(NM):
                                shifted_min(n0 + GI, h, True)


_INS = ["x", "p5_w", "w6t", "w8", "w10t", "dw_rev", "dw_b", "ln_g", "ln_b", "w1t", "b1", "w2t", "b2", "ls", "ident", "gmat", "edge"]


def kernel(**inputs):
    import numpy as np
    import concourse.bacc as bacc
    from concourse.bass_utils import run_bass_kernel_spmd

    a = {k: np.asarray(v) for k, v in inputs.items()}
    N, C, H, W = a["x"].shape
    col = lambda v: v.reshape(-1, 1)
    arrays = {
        "x": a["x"].reshape(N, C, H * W),
        "p5_w": a["L0_conv_p5_w"].reshape(C, H * W),
        "w6t": a["L0_conv_w6"].T,
        "w8": a["L0_conv_w8"].reshape(C // 2, -1),
        "w10t": a["L0_conv_w10"].T.reshape(C // 2, 3, C),
        "dw_rev": a["L1_conv_dw_w"].reshape(C, -1)[:, ::-1],
        "dw_b": a["L1_conv_dw_b"],
        "ln_g": col(a["L1_conv_ln_g"]),
        "ln_b": col(a["L1_conv_ln_b"]),
        "w1t": a["L1_conv_w1"].T,
        "b1": a["L1_conv_b1"].reshape(-1, C).T,
        "w2t": a["L1_conv_w2"].T,
        "b2": col(a["L1_conv_b2"]),
        "ls": col(a["L1_conv_ls"]),
        "ident": np.eye(C, dtype=np.float32),
        "gmat": np.kron(np.eye(32, dtype=np.float32), np.full((C // 32, C // 32), 32 / C, np.float32)),
    }
    cols = np.r_[0:6, W - 6:W]
    inside = np.stack([(cols + 3 * j - 6 >= 0) & (cols + 3 * j - 6 < W) for j in range(5)])
    arrays["edge"] = np.tile(inside, (24, 1)).astype(np.float32)
    nc = bacc.Bacc("TRN2", target_bir_lowering=False, num_devices=1)
    named, args = {}, []
    for name in _INS:
        v = np.ascontiguousarray(arrays[name])
        named[f"in_{name}"] = v
        args.append(nc.dram_tensor(f"in_{name}", v.shape, mybir.dt.from_np(v.dtype), kind="ExternalInput").ap())
    out = nc.dram_tensor("out_0", (N, C, H * W), F32, kind="ExternalOutput").ap()
    build(nc, *args, out)
    r = run_bass_kernel_spmd(nc, [named], core_ids=[0])
    return r.results[0]["out_0"].reshape(N, C, H, W)
```
